# Optimizing a Trainium2 kernel written in Bass

```python
import numpy as np
import jax
import jax.numpy as jnp

def _softmax(x, axis=-1):
    return jax.nn.softmax(x, axis=axis)

def _gelu(x):
    return jax.nn.gelu(x, approximate=True)

def _silu(x):
    return jax.nn.silu(x)

def _sigmoid(x):
    return jax.nn.sigmoid(x)

def _layernorm(x, axis=-1, eps=1e-05):
    m = jnp.mean(x, axis=axis, keepdims=True)
    v = jnp.var(x, axis=axis, keepdims=True)
    return (x - m) / jnp.sqrt(v + eps)

def _scatter_add(tgt, idx, src, axis=0):
    return tgt.at[idx].add(src)

def _segment_sum(src, seg, n):
    return jax.ops.segment_sum(src, seg, n)
kernel_name = 'mk_prb_d1_jaxref_r8_7af6af'

def setup_inputs(seed: int=0):
    np.random.seed(seed)
    _w = jnp.asarray

    def _L0_attn_setup():
        import jax, jax.numpy as jnp
        import numpy as np
        B, T, C = (2, 256, 256)
        H, KVH = (8, 2)
        DH = C // H
        ROPE_BASE = 10000.0
        NEG = -1000000000.0

        def _rope_tables(t, d):
            inv = 1.0 / ROPE_BASE ** (jnp.arange(0, d, 2, dtype=jnp.float32) / d)
            f = jnp.arange(t, dtype=jnp.float32)[:, None] * inv[None, :]
            cos = jnp.concatenate([jnp.cos(f), jnp.cos(f)], axis=-1)
            sin = jnp.concatenate([jnp.sin(f), jnp.sin(f)], axis=-1)
            return (cos, sin)

        def _apply_rope(x, cos, sin):
            d = x.shape[-1] // 2
            x1, x2 = (x[..., :d], x[..., d:])
            rot = jnp.concatenate([-x2, x1], axis=-1)
            return x * cos + rot * sin

        def _head_dirs():
            trig = np.array([[sx, sy, sz] for sx in (1.0, -1.0) for sy in (1.0, -1.0) for sz in (1.0, -1.0)], dtype=np.float32)
            return jnp.asarray(trig / np.sqrt(3.0))
        key = jax.random.key(seed)
        ks = jax.random.split(key, 6)
        s = 0.02
        return {'x': jax.random.normal(ks[0], (B, T, C), jnp.float32), 'Wq': jax.random.normal(ks[1], (C, H * DH), jnp.float32) * s, 'Wk': jax.random.normal(ks[2], (C, KVH * DH), jnp.float32) * s, 'Wv': jax.random.normal(ks[3], (C, KVH * DH), jnp.float32) * s, 'Wo': jax.random.normal(ks[4], (C, C), jnp.float32) * s, 'head_scales': jax.random.normal(ks[5], (H,), jnp.float32) * 0.1}
    _L0_attn_in = _L0_attn_setup()

    def _L0_ffn_setup():
        import jax, jax.numpy as jnp
        import numpy as np
        TARGET_SPARSITY = 0.9
        LN_EPS = 1e-05

        def ternary_quant(W):
            scale = jnp.mean(jnp.abs(W))
            q = jnp.clip(jnp.round(W / (scale + 1e-08)), -1.0, 1.0) * scale
            return W + jax.lax.stop_gradient(q - W)

        def layernorm(x, gamma, beta):
            mu = jnp.mean(x, axis=-1, keepdims=True)
            var = jnp.var(x, axis=-1, keepdims=True)
            return (x - mu) * jax.lax.rsqrt(var + LN_EPS) * gamma + beta
        key = jax.random.key(seed)
        ks = jax.random.split(key, 3)
        B, S, D, N = (4, 256, 256, 1024)
        x = jax.random.normal(ks[0], (B, S, D), dtype=jnp.float32)
        W_syn = jax.random.normal(ks[1], (N, D), dtype=jnp.float32) * (1.0 / np.sqrt(D))
        b_syn = jnp.zeros((N,), dtype=jnp.float32)
        W_out = jax.random.normal(ks[2], (D, N), dtype=jnp.float32) * (1.0 / np.sqrt(N))
        b_out = jnp.zeros((D,), dtype=jnp.float32)
        gamma = jnp.ones((D,), dtype=jnp.float32)
        beta = jnp.zeros((D,), dtype=jnp.float32)
        return {'x': x, 'W_syn': W_syn, 'b_syn': b_syn, 'W_out': W_out, 'b_out': b_out, 'gamma': gamma, 'beta': beta}
    _L0_ffn_in = _L0_ffn_setup()
    _d = {'L0_attn_x': _L0_attn_in['x'], 'L0_attn_Wq': _L0_attn_in['Wq'], 'L0_attn_Wk': _L0_attn_in['Wk'], 'L0_attn_Wv': _L0_attn_in['Wv'], 'L0_attn_Wo': _L0_attn_in['Wo'], 'L0_attn_head_scales': _L0_attn_in['head_scales'], 'L0_ffn_W_syn': _L0_ffn_in['W_syn'], 'L0_ffn_b_syn': _L0_ffn_in['b_syn'], 'L0_ffn_W_out': _L0_ffn_in['W_out'], 'L0_ffn_b_out': _L0_ffn_in['b_out'], 'L0_ffn_gamma': _L0_ffn_in['gamma'], 'L0_ffn_beta': _L0_ffn_in['beta']}
    _x0 = _d['L0_attn_x']
    _d['L0_attn_x'] = jax.random.normal(jax.random.fold_in(jax.random.key(seed), 1), (1, 2048, 256), dtype=_x0.dtype)
    del _x0
    return _d

def reference(L0_attn_x, L0_attn_Wq, L0_attn_Wk, L0_attn_Wv, L0_attn_Wo, L0_attn_head_scales, L0_ffn_W_syn, L0_ffn_b_syn, L0_ffn_W_out, L0_ffn_b_out, L0_ffn_gamma, L0_ffn_beta):

    def _L0_attn_ref(x, Wq, Wk, Wv, Wo, head_scales):
        import jax, jax.numpy as jnp
        import numpy as np
        B, T, C = (2, 256, 256)
        H, KVH = (8, 2)
        DH = C // H
        ROPE_BASE = 10000.0
        NEG = -1000000000.0

        def _rope_tables(t, d):
            inv = 1.0 / ROPE_BASE ** (jnp.arange(0, d, 2, dtype=jnp.float32) / d)
            f = jnp.arange(t, dtype=jnp.float32)[:, None] * inv[None, :]
            cos = jnp.concatenate([jnp.cos(f), jnp.cos(f)], axis=-1)
            sin = jnp.concatenate([jnp.sin(f), jnp.sin(f)], axis=-1)
            return (cos, sin)

        def _apply_rope(x, cos, sin):
            d = x.shape[-1] // 2
            x1, x2 = (x[..., :d], x[..., d:])
            rot = jnp.concatenate([-x2, x1], axis=-1)
            return x * cos + rot * sin

        def _head_dirs():
            trig = np.array([[sx, sy, sz] for sx in (1.0, -1.0) for sy in (1.0, -1.0) for sz in (1.0, -1.0)], dtype=np.float32)
            return jnp.asarray(trig / np.sqrt(3.0))
        Bn, Tn, Cn = x.shape
        q = (x @ Wq).reshape(Bn, Tn, H, DH).transpose(0, 2, 1, 3)
        k = (x @ Wk).reshape(Bn, Tn, KVH, DH).transpose(0, 2, 1, 3)
        v = (x @ Wv).reshape(Bn, Tn, KVH, DH).transpose(0, 2, 1, 3)
        cos, sin = _rope_tables(Tn, DH)
        q = _apply_rope(q, cos, sin)
        k = _apply_rope(k, cos, sin)
        rep = H // KVH
        k = jnp.repeat(k, rep, axis=1)
        v = jnp.repeat(v, rep, axis=1)
        causal = jnp.tril(jnp.ones((Tn, Tn), dtype=bool))
        scale = DH ** (-0.5)
        scores = jnp.einsum('bhtd,bhsd->bhts', q, k) * scale
        scores = jnp.where(causal, scores, NEG)
        out = jax.nn.softmax(scores, axis=-1) @ v
        dirs = _head_dirs()
        qp = jnp.einsum('bhtd,hd->bht', q[..., :3], dirs)
        kp = jnp.einsum('bhsd,hd->bhs', k[..., :3], dirs)
        geo = qp[..., :, None] * kp[..., None, :]
        geo = jnp.where(causal, geo, NEG)
        geo_out = jax.nn.softmax(geo, axis=-1) @ v
        scales = head_scales[None, :, None, None]
        out = out + scales * jax.lax.stop_gradient(geo_out - out)
        out = out.transpose(0, 2, 1, 3).reshape(Bn, Tn, Cn)
        return out @ Wo

    def _L0_ffn_ref(x, W_syn, b_syn, W_out, b_out, gamma, beta):
        import jax, jax.numpy as jnp
        import numpy as np
        TARGET_SPARSITY = 0.9
        LN_EPS = 1e-05

        def ternary_quant(W):
            scale = jnp.mean(jnp.abs(W))
            q = jnp.clip(jnp.round(W / (scale + 1e-08)), -1.0, 1.0) * scale
            return W + jax.lax.stop_gradient(q - W)

        def layernorm(x, gamma, beta):
            mu = jnp.mean(x, axis=-1, keepdims=True)
            var = jnp.var(x, axis=-1, keepdims=True)
            return (x - mu) * jax.lax.rsqrt(var + LN_EPS) * gamma + beta
        B, S, D = x.shape
        N = W_syn.shape[0]
        x_flat = x.reshape(-1, D)
        z = x_flat @ ternary_quant(W_syn).T + b_syn
        k = max(1, int(N * (1.0 - TARGET_SPARSITY)))
        topv, _ = jax.lax.top_k(z, k)
        thresh = topv[:, -1:]
        hidden = jnp.where(z >= thresh, jax.nn.relu(z), 0.0)
        out = hidden @ ternary_quant(W_out).T + b_out
        out = out.reshape(B, S, D)
        return layernorm(x + out, gamma, beta)
    x = L0_attn_x
    xn = _layernorm(x, axis=-1)
    x = x + _L0_attn_ref(xn, L0_attn_Wq, L0_attn_Wk, L0_attn_Wv, L0_attn_Wo, L0_attn_head_scales) + _L0_ffn_ref(xn, L0_ffn_W_syn, L0_ffn_b_syn, L0_ffn_W_out, L0_ffn_b_out, L0_ffn_gamma, L0_ffn_beta)
    return x

_drawn_inputs = setup_inputs


def setup_inputs(seed=0):
    import zlib

    import numpy as np

    out = dict(_drawn_inputs(seed))
    spreads = {'L0_ffn_b_syn': (0.0, 0.485),
     'L0_ffn_b_out': (0.0, 0.425),
     'L0_ffn_gamma': (1.0, 0.2),
     'L0_ffn_beta': (0.0, 0.429)}
    factors = {'L0_attn_Wq': 8.0,
     'L0_attn_Wk': 8.0,
     'L0_attn_Wv': 8.0,
     'L0_attn_Wo': 8.0,
     'L0_attn_head_scales': 8.0}
    for name, (base, spread) in spreads.items():
        noise = np.random.default_rng([zlib.crc32(name.encode()), seed]).standard_normal(out[name].shape)
        drawn = base * np.exp(spread * noise) if base else spread * noise
        out[name] = jnp.asarray(drawn.astype(out[name].dtype))
    for name, factor in factors.items():
        out[name] = (out[name] * factor).astype(out[name].dtype)
    return out
```

```python
from contextlib import ExitStack

import concourse.bass as bass
from concourse import mybir

F32 = mybir.dt.float32
F32R = mybir.dt.float32r
ALU = mybir.AluOpType
ACT = mybir.ActivationFunctionType
AX = mybir.AxisListType

P = 128
T, C = 2048, 256
H, G, D = 8, 2, 32
HG = H // G
HALF = D // 2
CHUNK = 512
NCH = T // CHUNK
NT = T // P
TPC = CHUNK // P
KC = C // P
N = 1024
NN = N // P
KTOP = max(1, int(N * (1.0 - 0.9)))
TOP_ROUNDS = (KTOP + 7) // 8
QKV = (H + 2 * G) * D
QK = (H + G) * D
STK = 3 * D
SROWS = STK + 2
GROWS = 5
ATT_SCALE = float(D) ** -0.5
LN_EPS = 1e-5
HI_ROW = 64
MASKED = -1e30


def build_plan():
    def side_units(item):
        k, a = item[0], item[1:]
        if k == "prep":
            return [(("xT",) + a, 150, 350, True), (("qkv",) + a, 1300, 2600, True),
                    (("qT", a[0], 0), 300, 600, True), (("qT", a[0], 1), 300, 600, False),
                    (("kT",) + a, 250, 600, False)]
        if k == "geo":
            return []
        if k == "max":
            t = a[0]
            return [(("S",) + a + (p,), 230, 130 + (CHUNK if p < t // TPC else (t % TPC + 1) * P), False)
                    for p in range(t // TPC + 1)]
        if k == "mrow":
            return [(("mT",) + a, 250, 1300, True)]
        if k == "quant":
            return [(("wsum",) + a, 100, 6000, True)] + [(("wT", a[0], i), 300, 600, True) for i in range(4)]
        if k == "ffn_up":
            return [(("xsT",) + a, 150, 800, True), (("z", a[0], 0), 1100, 600, True), (("z", a[0], 1), 1100, 28000, False)]
        if k == "ffn_down":
            return [(("hT", a[0], 0), 300, 1200, True), (("hT", a[0], 1), 300, 1200, False), (("fo",) + a, 1800, 1500, True)]
        if k == "oproj":
            return [(("o",) + a, 900, 400, False)]
        return []

    side = []
    for c in range(NCH):
        side += [("load", c)] if c == 0 else []
        side += [("prep", t) for t in range(TPC * c, TPC * c + TPC)]
        side += [("geo", c)]
        for t in range(TPC * c, TPC * c + TPC):
            side += [("max", t, h) for h in range(H)] + [("mx", t)]
        side += [("mrow", c), ("chunk_ready", c)]
    side += [("quant", 0), ("quant", 1)]
    for t in range(NT):
        side += [("ffn_up", t), ("ffn_down", t)]

    attention = []
    for c in range(NCH):
        for g in range(G):
            for kind in range(2):
                js = TPC * (c + 1)
                steps = []
                for j in range(js):
                    ncol = CHUNK - max(0, j - TPC * c) * P
                    pv = 470 * ncol // CHUNK * 2
                    s = 430 * ncol // CHUNK
                    steps.append(([("score", c, g, kind, j, 0), s], [("score", c, g, kind, j, 1), s],
                                  [("values", c, g, kind, j), pv], [("sums", c, g, kind, j), pv]))
                out = [steps[0][0], steps[0][1]]
                for j in range(js):
                    if j + 1 < js:
                        out += [steps[j + 1][0], steps[j][2], steps[j + 1][1], steps[j][3]]
                    else:
                        out += [steps[j][2], steps[j][3]]
                out += [[("epilogue", c, g, kind), 0]]
                attention += out
        attention += [[("attended", c), 0]]

    plan, units = [], {}
    pe, dve = 0.0, 0.0
    freed = [0.0, 0.0]
    ready = set()
    ai = 0
    si = 0
    pending = []
    late = []
    need = {0: 0, 1: 1, 2: 2, 3: 3}
    while ai < len(attention) or si < len(side) or pending or late:
        if not pending:
            if late and (late[0][0] <= pe or ai >= len(attention)):
                item = late.pop(0)[1]
                plan.append(item)
                pending = side_units(item)
            elif si < len(side):
                item = side[si]
                si += 1
                plan.append(item)
                if item[0] == "chunk_ready":
                    ready.add(item[1])
                pending = side_units(item)
                if not pending:
                    if item[0] == "geo":
                        dve += 7000
                    continue
        can_attend = ai < len(attention) and attention[ai][0][1] in ready
        if pending:
            name, pe_ns, dve_ns, after = pending[0]
            n = len(units)
            at = max(freed[n % 2], dve if after else 0.0)
            if at <= pe or not can_attend:
                units[name] = n
                plan.append(("unit",) + name)
                pe = max(pe, at) + pe_ns
                dve = max(dve, pe + 100) + dve_ns
                freed[n % 2] = dve
                pending.pop(0)
                continue
        if not can_attend:
            continue
        item, ns = attention[ai]
        ai += 1
        plan.append(item)
        pe += ns
        if item[0] == "epilogue":
            dve = max(dve, pe) + 1300
        if item[0] == "attended":
            late += [(pe + 12000, ("oproj", t)) for t in range(TPC * item[1], TPC * item[1] + TPC)]
    return plan, units


def attention_and_ternary_ffn(nc, x, Wq, Wk, Wv, Wo, head_scales, W_syn, b_syn, W_out, b_out, gamma, beta,
                              cos_table, sin_table, dirs_table, out):
    plan, unit = build_plan()
    order = {item: i for i, item in enumerate(plan)}
    ffn_last = {t: order[("unit", "fo", t)] > order[("unit", "o", t)] for t in range(NT)}
    score_index = {it: n for n, it in enumerate(i for i in plan if i[0] == "score")}
    pv_index = {it[1:]: n for n, it in enumerate(i for i in plan if i[0] == "sums")}
    epi_index = {it[1:]: n for n, it in enumerate(i for i in plan if i[0] == "epilogue")}
    oproj_index = {it[2]: n for n, it in enumerate(i for i in plan if i[:2] == ("unit", "o"))}

    ctx = ExitStack()
    with ctx:
        def sb(name, shape, dt=F32):
            return ctx.enter_context(nc.sbuf_tensor(name, shape, dt))

        def pb(name, shape):
            return ctx.enter_context(nc.psum_tensor(name, shape, F32))

        def sem(name):
            return ctx.enter_context(nc.semaphore(name))

        res = sb("res", [P, NT, C])
        xn = sb("xn", [P, NT, C])
        w_qkv = sb("w_qkv", [P, KC, QKV])
        w_o = sb("w_o", [P, G, C])
        cos = sb("cos", [P, NT, D])
        sin = sb("sin", [P, NT, D])
        dirs = sb("dirs", [P, H, 3])
        all_scales = sb("all_scales", [P, H])
        scale_h = sb("scale_h", [P, G])
        q_nat = sb("q_nat", [P, H, STK], F32R)
        k_nat = sb("k_nat", [P, G, STK], F32R)
        geo_prod = sb("geo_prod", [P, 2, H, 3])
        geo_nat = sb("geo_nat", [P, 2, H])
        q_stack = sb("q_stack", [SROWS, 2, H, CHUNK], F32R)
        k_stack = sb("k_stack", [SROWS, G, T], F32R)
        q_geo = sb("q_geo", [P, 2, G, CHUNK], F32R)
        k_geo = sb("k_geo", [P, G, T], F32R)
        head_rows = sb("head_rows", [HI_ROW + 1, 2, CHUNK])
        geo_row = head_rows[0:H]
        b_up = head_rows[HI_ROW:HI_ROW + 1].rearrange("p a n -> p (a n)")
        geo_split = sb("geo_split", [32 + H, 2, CHUNK], F32R)
        geo_hi, geo_lo = geo_split[0:H], geo_split[32:32 + H]
        run_max = sb("run_max", [H, CHUNK])
        run_min = sb("run_min", [H, CHUNK])
        run_end = sb("run_end", [H, 2])
        maxima = sb("maxima", [96 + H, CHUNK], F32R)
        gm_hi, gm_lo, m_hi, m_lo = (maxima[32 * i:32 * i + H] for i in range(4))
        piece_max = sb("piece_max", [P, H, NCH])
        row_max = sb("row_max", [P, TPC, H])
        v_nat = sb("v_nat", [P, NT, G, D])
        ones = sb("ones", [P, P])
        probs = sb("probs", [P, 2, HG, CHUNK])
        o_raw = sb("o_raw", [P, CHUNK])
        d_raw = sb("d_raw", [P, CHUNK])
        mixed = sb("mixed", [P, G, CHUNK])
        minus_half = sb("minus_half", [P, TPC])
        ident = sb("ident", [P, P])
        ident_r = sb("ident_r", [P, P], F32R)
        xb = sb("xb", [P, C])
        mask = xb[:].rearrange("p (a n) -> p a n", a=2)
        mask_r = sb("mask_r", [P, 2, P], F32R)
        stats = sb("stats", [P, 6])
        mean_var = sb("mean_var", [P, TPC, 2])
        rstd = sb("rstd", [P, TPC])
        w_abs = sb("w_abs", [P, 1])
        w_scale = sb("w_scale", [P, 2])
        w_cut = sb("w_cut", [P, 2])
        up_T = sb("up_T", [P, KC, N], F32R)
        down_T = sb("down_T", [P, NN, C], F32R)
        b_up_r = sb("b_up_r", [HI_ROW + 1, N], F32R)
        ones_r = sb("ones_r", [HI_ROW + 1, P], F32R)
        b_down = sb("b_down", [P, C])
        gam = sb("gam", [P, C])
        bet = sb("bet", [P, C])
        xs_hi = sb("xs_hi", [P, KC, P], F32R)
        xs_lo = sb("xs_lo", [P, KC, P], F32R)
        z_work = sb("z_work", [P, 2, N])
        z, work = z_work[:, 0], z_work[:, 1]
        rot_a, rot_b = z[:, 0:QK], z[:, QK:2 * QK]
        qk = z[:, 2 * QK:3 * QK]
        xnT = work[:, 0:C].rearrange("p (k t) -> p k t", k=KC)
        w_raw = z_work[:].rearrange("p a n -> p (a n)")
        top8 = sb("top8", [P, TOP_ROUNDS, 8])
        h_split = sb("h_split", [P, 2, NN, P], F32R)
        h_hi, h_lo = h_split[:, 0], h_split[:, 1]
        w_neg = h_split[:].rearrange("p a n t -> p (a n t)")
        y = sb("y", [P, C])
        y_stats = sb("y_stats", [P, 6])
        y_mv = sb("y_mv", [P, 2])
        y_rstd = sb("y_rstd", [P, 1])

        side = pb("side", [P, 2, CHUNK])
        scores = pb("scores", [P, 2, 2, CHUNK])
        acc = pb("acc", [P, 2, CHUNK])

        x_in = [sem(f"x_in{c}") for c in range(NCH)]
        w_in = sem("w_in")
        up_in = sem("up_in")
        down_in = sem("down_in")
        const_ready = sem("const_ready")
        pool_step = sem("pool_step")
        dve_step = sem("dve_step")
        side_full = sem("side_full")
        side_free = [sem("side_free0"), sem("side_free1")]
        var_ready = sem("var_ready")
        rstd_ready = sem("rstd_ready")
        masks_ready = sem("masks_ready")
        xn_ready = sem("xn_ready")
        nat_ready = sem("nat_ready")
        mx_ready = sem("mx_ready")
        geo_ready = sem("geo_ready")
        geo_in = [sem(f"geo_in{c}") for c in range(NCH)]
        m_in = [sem(f"m_in{c}") for c in range(NCH)]
        score_full = sem("score_full")
        probs_ready = sem("probs_ready")
        probs_used = sem("probs_used")
        acc_full = sem("acc_full")
        raw_ready = sem("raw_ready")
        raw_free = sem("raw_free")
        mixed_ready = sem("mixed_ready")
        quant_ready = sem("quant_ready")
        hidden_ready = sem("hidden_ready")
        xb_ready = sem("xb_ready")
        y_ready = sem("y_ready")
        ffn_added = sem("ffn_added")
        stored = sem("stored")

        block = ctx.enter_context(nc.Block())

        def consumed(eng, n):
            eng.wait_ge(side_free[n % 2], n // 2 + 1)

        def bank(name):
            return side[:, unit[name] % 2]

        x_rows = x.rearrange("o (c i p) d -> c p (o i) d", p=P, i=TPC)
        out_rows = out.rearrange("o (t p) d -> t p (o d)", p=P)
        N_W_IN = 16 * 12
        N_CONSTS = 10

        @block.sync
        def _(sp):
            sp.dma_start(res[:, 0:TPC], x_rows[0]).then_inc(x_in[0], 16)
            for w, at in ((Wq, 0), (Wk, H * D), (Wv, QK)):
                sp.dma_start(w_qkv[:, :, at:at + w.shape[1]],
                             w.rearrange("(k p) n -> p k n", p=P)).then_inc(w_in, 16)
            sp.dma_start(cos[:], cos_table.rearrange("(t p) d -> p t d", p=P)).then_inc(w_in, 16)
            sp.dma_start(sin[:], sin_table.rearrange("(t p) d -> p t d", p=P)).then_inc(w_in, 16)
            sp.dma_start(dirs[:], dirs_table.rearrange("(o h) i -> o h i", o=1).broadcast_to([P, H, 3])).then_inc(w_in, 16)
            for c in range(1, NCH):
                sp.dma_start(res[:, TPC * c:TPC * c + TPC], x_rows[c]).then_inc(x_in[c], 16)
            sp.dma_start(w_o[:], Wo.rearrange("(g p) n -> p g n", p=P)).then_inc(w_in, 16)
            for t_, v_ in ((all_scales, head_scales), (b_down, b_out), (gam, gamma), (bet, beta)):
                sp.dma_start(t_[:], v_.rearrange("(o n) -> o n", o=1).broadcast_to([P, v_.shape[0]])).then_inc(w_in, 16)
            sp.dma_start(b_up, b_syn.rearrange("(o n) -> o n", o=1)).then_inc(w_in, 16)
            for item in plan:
                k = item[0]
                if k == "geo":
                    c = item[1]
                    b, cols = c % 2, slice(CHUNK * c, CHUNK * c + CHUNK)
                    sp.wait_ge(geo_ready, c + 1)
                    if c >= 2:
                        sp.wait_ge(acc_full, 2 * G * (c - 1))
                    for g in range(G):
                        hs_ = slice(HG * g, HG * g + HG)
                        for r, src in enumerate((geo_hi[hs_, 0], geo_lo[hs_, 0], geo_hi[hs_, 0])):
                            sp.dma_start(k_geo[r:r + 97:32, g, cols].bitcast(F32), src.bitcast(F32)).then_inc(geo_in[c], 16)
                        for r, src in enumerate((geo_hi[hs_, 1], geo_hi[hs_, 1], geo_lo[hs_, 1],
                                                 gm_hi[hs_], gm_lo[hs_])):
                            sp.dma_start(q_geo[r:r + 97:32, b, g, :].bitcast(F32), src.bitcast(F32)).then_inc(geo_in[c], 16)
                if k == "chunk_ready":
                    c = item[1]
                    consumed(sp, unit[("mT", c)])
                    for r, src in enumerate((m_hi, m_lo)):
                        for h in range(H):
                            sp.dma_start(q_stack[STK + r:STK + r + 1, c % 2, h, :].bitcast(F32),
                                         src[h:h + 1, :].bitcast(F32)).then_inc(m_in[c], 16)
                if item == ("quant", 0):
                    sp.wait_ge(nat_ready, NT)
                    sp.dma_start(w_raw.rearrange("p (a n) -> p a n", a=NN),
                                 W_syn.rearrange("(a p) n -> p a n", p=P)).then_inc(up_in, 16)
                if item == ("quant", 1):
                    sp.wait_ge(side_free[unit[("wT", 0, 3)] % 2], unit[("wT", 0, 3)] // 2 + 1)
                    sp.dma_start(w_raw.rearrange("p (a n) -> p a n", a=KC),
                                 W_out.rearrange("(a p) n -> p a n", p=P)).then_inc(down_in, 16)
                if k == "unit" and item[1] in ("o", "fo"):
                    t = item[2]
                    if ffn_last[t] == (item[1] == "fo"):
                        if ffn_last[t]:
                            sp.wait_ge(ffn_added, t + 1)
                        else:
                            consumed(sp, unit[("o", t)])
                        sp.dma_start(out_rows[t], res[:, t]).then_inc(stored, 16)
            sp.wait_ge(stored, 16 * NT)

        @block.gpsimd
        def _(pool):
            steps = [0]

            def link(ins):
                steps[0] += 1
                ins.then_inc(pool_step, 1)
                pool.wait_ge(pool_step, steps[0])

            consts = [0]

            def constant(ins):
                consts[0] += 1
                ins.then_inc(const_ready, 1)
                pool.wait_ge(const_ready, consts[0])

            constant(nc.gpsimd.memset(ident[:], 0.0))
            constant(nc.gpsimd.affine_select(out=ident[:], in_=ident[:], compare_op=ALU.not_equal, fill=1.0, base=0,
                                             pattern=[[-1, P]], channel_multiplier=1))
            constant(nc.gpsimd.memset(minus_half[:], -0.5))
            constant(nc.gpsimd.memset(xb[:], 0.0))
            constant(nc.gpsimd.affine_select(out=mask[:, 0], in_=mask[:, 0], compare_op=ALU.is_ge, fill=MASKED, base=0,
                                             pattern=[[1, P]], channel_multiplier=-1))
            constant(nc.gpsimd.affine_select(out=mask[:, 1], in_=mask[:, 1], compare_op=ALU.is_ge, fill=MASKED, base=0,
                                             pattern=[[-1, P]], channel_multiplier=1))
            constant(nc.gpsimd.memset(ones[:], 1.0))
            constant(nc.gpsimd.memset(k_geo[:].bitcast(F32), -1.0))
            constant(nc.gpsimd.memset(k_stack[STK:SROWS].bitcast(F32), -1.0))
            constant(nc.gpsimd.memset(b_up_r[:].bitcast(F32), 0.0))

            for item in plan:
                k = item[0]
                if k == "prep" and item[1] % TPC == 0:
                    pool.wait_ge(var_ready, item[1] // TPC + 1)
                    nc.gpsimd.tensor_tensor(rstd[:], mean_var[:, :, 1], minus_half[:], ALU.pow).then_inc(rstd_ready, 1)
                if k == "epilogue":
                    c, g, kind = item[1:]
                    n = epi_index[item[1:]]
                    pool.wait_ge(raw_ready, 2 * (n + 1))
                    if n == 0:
                        pool.wait_ge(w_in, N_W_IN)
                        for h in range(HG):
                            rows = slice(D * h, D * h + D)
                            link(nc.gpsimd.tensor_copy(scale_h[rows, :], all_scales[rows].rearrange(
                                "p (g h) -> p g h", g=G)[:, :, h]))
                    if kind == 0:
                        if c >= 1:
                            pool.wait_ge(side_full, unit[("o", TPC * c - 1)] + 1)
                        nc.gpsimd.tensor_tensor(mixed[:, g], o_raw[:], d_raw[:], ALU.mult).then_inc(raw_free, 1)
                        pool.wait_ge(raw_free, n + 1)
                    else:
                        link(nc.gpsimd.tensor_tensor(o_raw[:], o_raw[:], d_raw[:], ALU.mult))
                        link(nc.gpsimd.tensor_tensor(o_raw[:], o_raw[:], mixed[:, g], ALU.subtract))
                        link(nc.gpsimd.tensor_scalar(o_raw[:], o_raw[:], scale_h[:, g:g + 1], None, ALU.mult))
                        link(nc.gpsimd.tensor_tensor(mixed[:, g], o_raw[:], mixed[:, g], ALU.add))
                        pool.nop().then_inc(raw_free, 1)
                        pool.nop().then_inc(mixed_ready, 1)
                if k == "unit" and item[1] == "xsT":
                    t = item[2]
                    if t >= 1:
                        pool.wait_ge(y_ready, t)
                    nc.gpsimd.tensor_tensor(xb[:], xn[:, t], b_down[:], ALU.add).then_inc(xb_ready, 1)
                if k == "unit" and item[1] == "fo":
                    t = item[2]
                    pool.wait_ge(y_ready, t + 1)
                    link(nc.gpsimd.tensor_tensor(y_rstd[:], y_mv[:, 1:2], minus_half[:, 0:1], ALU.pow))
                    link(nc.gpsimd.tensor_scalar(y[:], y[:], y_mv[:, 0:1], y_rstd[:, 0:1], ALU.subtract, ALU.mult))
                    link(nc.gpsimd.tensor_tensor(y[:], y[:], gam[:], ALU.mult))
                    link(nc.gpsimd.tensor_tensor(y[:], y[:], bet[:], ALU.add))
                    if ffn_last[t]:
                        consumed(pool, unit[("o", t)])
                    nc.gpsimd.tensor_tensor(res[:, t], res[:, t], y[:], ALU.add).then_inc(ffn_added, 1)

        @block.scalar
        def _(act):
            for item in plan:
                if item[0] != "score":
                    continue
                c, g, kind, j, pair = item[1:]
                n = score_index[item]
                off = max(0, j - TPC * c) * P
                slot = pv_index[(c, g, kind, j)]
                act.wait_ge(score_full, n + 1)
                if pair == 0 and slot >= 2:
                    act.wait_ge(probs_used, slot - 1)
                nc.scalar.activation(probs[:, slot % 2, 2 * pair:2 * pair + 2, off:], scores[:, n % 2, :, off:], ACT.Exp,
                                     scale=ATT_SCALE if kind == 0 else 1.0).then_inc(probs_ready, 1)

        @block.vector
        def _(dve):
            steps = [0]

            def mark(ins):
                steps[0] += 1
                ins.then_inc(dve_step, 1)

            def settle():
                dve.wait_ge(dve_step, steps[0])

            def link(ins):
                mark(ins)
                settle()

            def filled(name):
                dve.wait_ge(side_full, unit[name] + 1)
                return side[:, unit[name] % 2]

            def free(ins, name):
                ins.then_inc(side_free[unit[name] % 2], 1)

            def row_stats(c):
                dve.wait_ge(x_in[c], 16)
                for i in range(TPC):
                    link(nc.vector.bn_stats(stats[:], res[:, TPC * c + i]))
                    link(nc.vector.bn_aggr(mean_var[:, i, :], stats[:]))
                nc.vector.tensor_scalar(mean_var[:, :, 1], mean_var[:, :, 1], LN_EPS, None, ALU.add).then_inc(var_ready, 1)
                dve.wait_ge(rstd_ready, c + 1)
                for i in range(TPC):
                    nc.vector.tensor_scalar(xn[:, TPC * c + i], res[:, TPC * c + i], mean_var[:, i, 0:1],
                                            rstd[:, i:i + 1], ALU.subtract, ALU.mult).then_inc(xn_ready, 1)

            dve.wait_ge(const_ready, N_CONSTS)
            link(nc.vector.tensor_copy(ident_r[:], ident[:]))
            mark(nc.vector.tensor_copy(ones_r[:], ones[0:HI_ROW + 1, :]))
            mark(nc.vector.memset(run_end[:, 0:1], -3.0e38))
            mark(nc.vector.memset(run_end[:, 1:2], 3.0e38))
            nc.vector.tensor_copy(mask_r[:], mask).then_inc(masks_ready, 1)
            dve.wait_ge(masks_ready, 1)
            settle()

            for item in plan:
                k, a = item[0], item[1:]
                if k == "prep" and a[0] % TPC == 0:
                    row_stats(a[0] // TPC)
                if k == "unit" and a[0] == "xT":
                    pt = filled(a)
                    free(nc.vector.tensor_copy(xnT, pt[:, 0:C].rearrange("p (k t) -> p k t", k=KC)), a)
                if k == "unit" and a[0] == "qkv":
                    t = a[1]
                    if t == 0:
                        dve.wait_ge(w_in, N_W_IN)
                    pt = filled(a)
                    pq = pt[:, 0:QK].rearrange("p (h f i) -> p h f i", f=2, i=HALF)
                    rb = rot_b.rearrange("p (h f i) -> p h f i", f=2, i=HALF)
                    mark(nc.vector.tensor_tensor(rot_a.rearrange("p (h d) -> p h d", d=D),
                                                 pt[:, 0:QK].rearrange("p (h d) -> p h d", d=D),
                                                 cos[:, t:t + 1, :].broadcast_to([P, H + G, D]), ALU.mult))
                    for f in range(2):
                        mark(nc.vector.tensor_tensor(
                            rb[:, :, f], pq[:, :, 1 - f],
                            sin[:, t:t + 1, HALF * f:HALF * f + HALF].broadcast_to([P, H + G, HALF]), ALU.mult))
                    mark(nc.vector.tensor_copy(v_nat[:, t], pt[:, QK:QKV].rearrange("p (g d) -> p g d", g=G)))
                    settle()
                    nc.vector.tensor_tensor(qk, rot_a, rot_b, ALU.add).then_inc(side_free[unit[a] % 2], 1)
                    dve.wait_ge(side_free[unit[a] % 2], unit[a] // 2 + 1)
                    q = qk[:, 0:H * D].rearrange("p (h d) -> p h d", d=D)
                    kk = qk[:, H * D:QK].rearrange("p (g d) -> p g d", d=D)
                    mark(nc.vector.tensor_copy(q_nat[:, :, 0:D], q))
                    mark(nc.vector.tensor_copy(q_nat[:, :, D:2 * D], q))
                    mark(nc.vector.tensor_copy(k_nat[:, :, 0:D], kk))
                    mark(nc.vector.tensor_copy(k_nat[:, :, 2 * D:], kk))
                    mark(nc.vector.tensor_tensor(geo_prod[:, 1], q[:, :, 0:3], dirs[:], ALU.mult))
                    for g in range(G):
                        hs_ = slice(HG * g, HG * g + HG)
                        mark(nc.vector.tensor_tensor(geo_prod[:, 0, hs_], kk[:, g:g + 1, 0:3].broadcast_to([P, HG, 3]),
                                                     dirs[:, hs_], ALU.mult))
                    settle()
                    mark(nc.vector.tensor_tensor(q_nat[:, :, 2 * D:], q, q_nat[:, :, 0:D].bitcast(F32), ALU.subtract))
                    mark(nc.vector.tensor_tensor(k_nat[:, :, D:2 * D], kk, k_nat[:, :, 0:D].bitcast(F32), ALU.subtract))
                    nc.vector.tensor_reduce(geo_nat[:], geo_prod[:], AX.X, ALU.add).then_inc(nat_ready, 1)
                    settle()
                    dve.wait_ge(nat_ready, t + 1)
                if k == "unit" and a[0] == "qT":
                    t, half = a[1:]
                    c, col = t // TPC, t % TPC * P
                    pt = filled(a)
                    if half == 0 and t % TPC == 0 and c >= 2:
                        dve.wait_ge(acc_full, 2 * G * (c - 1))
                    free(nc.vector.tensor_copy(q_stack[0:STK, c % 2, 4 * half:4 * half + 4, col:col + P],
                                               pt[0:STK].rearrange("p (h t) -> p h t", t=P)), a)
                if k == "unit" and a[0] == "kT":
                    t = a[1]
                    col = t % TPC * P
                    pt = filled(a)
                    if t % TPC == 0 and t >= TPC:
                        dve.wait_ge(geo_in[t // TPC - 1], 16 * 8 * G)
                    mark(nc.vector.tensor_copy(k_stack[0:STK, :, P * t:P * t + P],
                                               pt[0:STK, 0:G * P].rearrange("p (g t) -> p g t", t=P)))
                    free(nc.vector.tensor_copy(geo_row[:, :, col:col + P],
                                               pt[0:H, G * P:G * P + 2 * P].rearrange("p (a t) -> p a t", t=P)), a)
                    settle()
                    consumed(dve, unit[a])
                if k == "geo":
                    c = a[0]
                    kp, qp = geo_row[:, 0], geo_row[:, 1]
                    mark(nc.vector.tensor_copy(geo_hi, geo_row))
                    mark(nc.vector.tensor_tensor_scan(run_max[:], kp, kp, run_end[:, 0:1], ALU.max, ALU.max))
                    mark(nc.vector.tensor_tensor_scan(run_min[:], kp, kp, run_end[:, 1:2], ALU.min, ALU.min))
                    settle()
                    mark(nc.vector.tensor_tensor(geo_lo, geo_row, geo_hi.bitcast(F32), ALU.subtract))
                    mark(nc.vector.tensor_copy(run_end[:, 0:1], run_max[:, CHUNK - 1:]))
                    mark(nc.vector.tensor_copy(run_end[:, 1:2], run_min[:, CHUNK - 1:]))
                    settle()
                    mark(nc.vector.tensor_tensor(run_max[:], run_max[:], qp, ALU.mult))
                    mark(nc.vector.tensor_tensor(run_min[:], run_min[:], qp, ALU.mult))
                    settle()
                    link(nc.vector.tensor_tensor(run_max[:], run_max[:], run_min[:], ALU.max))
                    link(nc.vector.tensor_copy(gm_hi, run_max[:]))
                    nc.vector.tensor_tensor(gm_lo, run_max[:], gm_hi.bitcast(F32), ALU.subtract).then_inc(geo_ready, 1)
                    dve.wait_ge(geo_ready, c + 1)
                if k == "unit" and a[0] == "S":
                    t, h, p = a[1:]
                    ncol = CHUNK if p < t // TPC else (t % TPC + 1) * P
                    pt = filled(a)
                    free(nc.vector.tensor_reduce(piece_max[:, h, p:p + 1], pt[:, 0:ncol], AX.X, ALU.max), a)
                if k == "mx":
                    t = a[0]
                    for back in range(min(2, H * (t // TPC + 1))):
                        consumed(dve, unit[("S", t, H - 1, t // TPC)] - back)
                    if t % TPC == 0 and t >= TPC:
                        dve.wait_ge(side_full, unit[("mT", t // TPC - 1)] + 1)
                    ins = nc.vector.tensor_reduce(row_max[:, t % TPC], piece_max[:, :, 0:t // TPC + 1], AX.X, ALU.max)
                    ins.then_inc(mx_ready, 1)
                    dve.wait_ge(mx_ready, t + 1)
                if k == "unit" and a[0] == "mT":
                    c = a[1]
                    pt = filled(a)
                    if c >= 1:
                        dve.wait_ge(m_in[c - 1], 16 * 2 * H)
                    link(nc.vector.tensor_copy(m_hi, pt[0:H]))
                    free(nc.vector.tensor_tensor(m_lo, pt[0:H], m_hi.bitcast(F32), ALU.subtract), a)
                if k == "epilogue":
                    n = epi_index[a]
                    dve.wait_ge(acc_full, n + 1)
                    if n >= 1:
                        dve.wait_ge(raw_free, n)
                    nc.vector.tensor_copy(o_raw[:], acc[:, 0]).then_inc(raw_ready, 1)
                    nc.vector.reciprocal(d_raw[:], acc[:, 1]).then_inc(raw_ready, 1)
                if k == "unit" and a[0] == "o":
                    t = a[1]
                    pt = filled(a)
                    if not ffn_last[t]:
                        dve.wait_ge(ffn_added, t + 1)
                    free(nc.vector.tensor_tensor(res[:, t], pt[:, 0:C], res[:, t], ALU.add), a)
                if k == "quant":
                    m = a[0]
                    dve.wait_ge(up_in if m == 0 else down_in, 16)
                    if m == 1:
                        consumed(dve, unit[("wT", 0, 3)])
                    nc.vector.tensor_reduce(w_abs[:], w_raw, AX.X, ALU.add,
                                            apply_absolute_value=True).then_inc(quant_ready, 1)
                if k == "unit" and a[0] == "wsum":
                    m = a[1]
                    pt = filled(a)
                    link(nc.vector.tensor_scalar(w_scale[:, m:m + 1], pt[:, 0:1], 1.0 / (N * C), None, ALU.mult))
                    link(nc.vector.tensor_scalar(w_cut[:, 0:1], w_scale[:, m:m + 1], 1e-8, 0.5, ALU.add, ALU.mult))
                    link(nc.vector.tensor_scalar(w_cut[:, 1:2], w_cut[:, 0:1], -1.0, None, ALU.mult))
                    link(nc.vector.tensor_scalar(w_neg, w_raw, w_cut[:, 1:2], None, ALU.is_lt))
                    free(nc.vector.scalar_tensor_tensor(w_neg, w_raw, w_cut[:, 0:1], w_neg.bitcast(F32), ALU.is_gt,
                                                        ALU.subtract), a)
                if k == "unit" and a[0] == "wT":
                    m, i = a[1:]
                    pt = filled(a)
                    if m == 0:
                        dst = up_T[:, i // 2, CHUNK * (i % 2):CHUNK * (i % 2) + CHUNK]
                        src = pt
                    else:
                        dst = down_T[:, 2 * i:2 * i + 2, :]
                        src = pt.rearrange("p (a n) -> p a n", a=2)
                    free(nc.vector.tensor_copy(dst, src), a)
                    if m == 0 and i == 3:
                        dve.wait_ge(w_in, N_W_IN)
                        link(nc.vector.tensor_copy(b_up_r[HI_ROW:HI_ROW + 1, :], b_up))
                        link(nc.vector.tensor_tensor(b_up_r[0:1, :], b_up, b_up_r[HI_ROW:HI_ROW + 1, :].bitcast(F32), ALU.subtract))
                if k == "unit" and a[0] == "xsT":
                    t = a[1]
                    pt = filled(a)
                    pt3 = pt[:, 0:C].rearrange("p (k t) -> p k t", k=KC)
                    link(nc.vector.tensor_scalar(xs_hi[:], pt3, w_scale[:, 0:1], None, ALU.mult))
                    free(nc.vector.scalar_tensor_tensor(xs_lo[:], pt3, w_scale[:, 0:1], xs_hi[:].bitcast(F32), ALU.mult,
                                                        ALU.subtract), a)
                if k == "unit" and a[0] == "z":
                    t, half = a[1:]
                    pt = filled(a)
                    free(nc.vector.tensor_scalar(z[:, CHUNK * half:CHUNK * half + CHUNK], pt, 0.0, None, ALU.max), a)
                    if half == 1:
                        for b in range(2):
                            consumed(dve, unit[("z", t, b)])
                        cur = z
                        for r in range(TOP_ROUNDS):
                            link(nc.vector.max(top8[:, r], cur))
                            if r < TOP_ROUNDS - 1:
                                link(nc.vector.match_replace(work, top8[:, r], cur, -1.0))
                            cur = work
                        last = (KTOP - 1) % 8
                        nc.vector.scalar_tensor_tensor(work, z, top8[:, TOP_ROUNDS - 1, last:last + 1], z,
                                                       ALU.is_ge, ALU.mult).then_inc(hidden_ready, 1)
                        dve.wait_ge(hidden_ready, t + 1)
                if k == "unit" and a[0] == "hT":
                    t, half = a[1:]
                    pt = filled(a).rearrange("p (a t) -> p a t", t=P)
                    s_ = slice(4 * half, 4 * half + 4)
                    link(nc.vector.tensor_copy(h_hi[:, s_], pt))
                    free(nc.vector.tensor_tensor(h_lo[:, s_], pt, h_hi[:, s_].bitcast(F32), ALU.subtract), a)
                if k == "unit" and a[0] == "fo":
                    t = a[1]
                    pt = filled(a)
                    dve.wait_ge(xb_ready, t + 1)
                    if t >= 1:
                        dve.wait_ge(ffn_added, t)
                    link(nc.vector.scalar_tensor_tensor(y[:], pt[:, 0:C], w_scale[:, 1:2], xb[:], ALU.mult, ALU.add))
                    free(nc.vector.bn_stats(y_stats[:], y[:]), a)
                    consumed(dve, unit[a])
                    link(nc.vector.bn_aggr(y_mv[:], y_stats[:]))
                    nc.vector.tensor_scalar(y_mv[:, 1:2], y_mv[:, 1:2], LN_EPS, None, ALU.add).then_inc(y_ready, 1)
                    dve.wait_ge(y_ready, t + 1)

        @block.tensor
        def _(pe):
            pe.wait_ge(const_ready, N_CONSTS)
            pe.wait_ge(masks_ready, 1)
            for item in plan:
                k, a = item[0], item[1:]
                if k == "unit":
                    n = unit[a]
                    pt = side[:, n % 2]
                    if n >= 2:
                        consumed(pe, n - 2)
                    if a[0] == "xT":
                        t = a[1]
                        pe.wait_ge(xn_ready, t + 1)
                        for i in range(KC):
                            last = nc.tensor.transpose(pt[:, P * i:P * i + P], xn[:, t, P * i:P * i + P], ident[:])
                    if a[0] == "qkv":
                        t = a[1]
                        consumed(pe, unit[("xT", t)])
                        if t == 0:
                            pe.wait_ge(w_in, N_W_IN)
                        for i in range(KC):
                            last = nc.tensor.matmul(pt[:, 0:QKV], xnT[:, i], w_qkv[:, i], start=(i == 0), stop=(i == KC - 1))
                    if a[0] == "qT":
                        t, half = a[1:]
                        pe.wait_ge(nat_ready, t + 1)
                        for i in range(4):
                            last = nc.tensor.transpose(pt[0:STK, P * i:P * i + P], q_nat[:, 4 * half + i].bitcast(F32), ident[:])
                    if a[0] == "kT":
                        t = a[1]
                        for g in range(G):
                            nc.tensor.transpose(pt[0:STK, P * g:P * g + P], k_nat[:, g].bitcast(F32), ident[:])
                        for i in range(2):
                            last = nc.tensor.transpose(pt[0:H, P * (G + i):P * (G + i) + P], geo_nat[:, i], ident[:])
                    if a[0] == "S":
                        t, h, p = a[1:]
                        c, b, col = t // TPC, t // TPC % 2, t % TPC * P
                        if h == 0 and p == 0:
                            for back in range(3):
                                consumed(pe, unit[("kT", TPC * c + TPC - 1)] - back)
                        full = p < c
                        ncol = CHUNK if full else col + P
                        last = nc.tensor.matmul(pt[:, 0:ncol], q_stack[0:STK, b, h, col:col + P],
                                                k_stack[0:STK, h // HG, CHUNK * p:CHUNK * p + ncol], start=True, stop=full)
                        if not full:
                            last = nc.tensor.matmul(pt[:, col:col + P], ident_r[:], mask_r[:, 1], start=False, stop=True)
                    if a[0] == "mT":
                        c = a[1]
                        pe.wait_ge(mx_ready, TPC * (c + 1))
                        for i in range(TPC):
                            last = nc.tensor.transpose(pt[0:H, P * i:P * i + P], row_max[:, i], ident[:])
                    if a[0] == "wsum":
                        pe.wait_ge(quant_ready, a[1] + 1)
                        last = nc.tensor.matmul(pt[:, 0:1], ones[:], w_abs[:], start=True, stop=True)
                    if a[0] == "wT":
                        m, i = a[1:]
                        consumed(pe, unit[("wsum", m)])
                        for q in range(4):
                            if m == 0:
                                nt = 4 * (i % 2) + q
                                at = nt * C + (i // 2) * P
                            else:
                                nt, dt_ = 2 * i + q // 2, q % 2
                                at = dt_ * N + nt * P
                            last = nc.tensor.transpose(pt[:, P * q:P * q + P], w_neg[:, at:at + P].bitcast(F32), ident[:])
                    if a[0] == "xsT":
                        t = a[1]
                        for i in range(KC):
                            last = nc.tensor.transpose(pt[:, P * i:P * i + P], xn[:, t, P * i:P * i + P], ident[:])
                    if a[0] == "z":
                        t, half = a[1:]
                        consumed(pe, unit[("xsT", t)])
                        cols = slice(CHUNK * half, CHUNK * half + CHUNK)
                        for i in range(KC):
                            nc.tensor.matmul(pt, xs_hi[:, i], up_T[:, i, cols], start=(i == 0), stop=False)
                            nc.tensor.matmul(pt, xs_lo[:, i], up_T[:, i, cols], start=False, stop=False)
                        last = nc.tensor.matmul(pt, ones_r[:], b_up_r[:, cols], start=False, stop=True)
                    if a[0] == "hT":
                        t, half = a[1:]
                        pe.wait_ge(hidden_ready, t + 1)
                        for i in range(4):
                            at = P * (4 * half + i)
                            last = nc.tensor.transpose(pt[:, P * i:P * i + P], work[:, at:at + P], ident[:])
                    if a[0] == "fo":
                        t = a[1]
                        for half in range(2):
                            consumed(pe, unit[("hT", t, half)])
                        for i in range(NN):
                            nc.tensor.matmul(pt[:, 0:C], h_hi[:, i], down_T[:, i], start=(i == 0), stop=False)
                            last = nc.tensor.matmul(pt[:, 0:C], h_lo[:, i], down_T[:, i], start=False, stop=(i == NN - 1))
                    if a[0] == "o":
                        t = a[1]
                        c, col = t // TPC, t % TPC * P
                        pe.wait_ge(mixed_ready, G * (c + 1))
                        for g in range(G):
                            last = nc.tensor.matmul(pt[:, 0:C], mixed[:, g, col:col + P], w_o[:, g], start=(g == 0), stop=(g == G - 1))
                    last.then_inc(side_full, 1)
                if k == "score":
                    c, g, kind, j, pair = a
                    n = score_index[item]
                    b = c % 2
                    off = max(0, j - TPC * c) * P
                    if n >= 2:
                        pe.wait_ge(probs_ready, n - 1)
                    if g == 0 and j == 0 and pair == 0:
                        if kind == 0:
                            pe.wait_ge(m_in[c], 16 * 2 * H)
                        else:
                            pe.wait_ge(geo_in[c], 16 * 8 * G)
                    diagonal = j >= TPC * c
                    for i in range(2):
                        h = 2 * pair + i
                        dst = scores[:, n % 2, i]
                        if kind == 0:
                            last = nc.tensor.matmul(dst[:, off:], k_stack[:, g, P * j:P * j + P],
                                                    q_stack[:, b, HG * g + h, off:], start=True, stop=not diagonal)
                        else:
                            last = nc.tensor.matmul(dst[:, off:], k_geo[32 * h:32 * h + GROWS, g, P * j:P * j + P],
                                                    q_geo[32 * h:32 * h + GROWS, b, g, off:], start=True, stop=not diagonal)
                    if diagonal:
                        for i in range(2):
                            last = nc.tensor.matmul(scores[:, n % 2, i, off:off + P], ident_r[:], mask_r[:, 0],
                                                    start=False, stop=True)
                    last.then_inc(score_full, 1)
                if k in ("values", "sums"):
                    c, g, kind, j = a
                    slot = pv_index[a]
                    off = max(0, j - TPC * c) * P
                    first, end = j == 0, j == TPC * (c + 1) - 1
                    if k == "values":
                        pe.wait_ge(probs_ready, score_index[("score", c, g, kind, j, 1)] + 1)
                        n = epi_index[(c, g, kind)]
                        if first and n >= 1:
                            pe.wait_ge(raw_ready, 2 * n)
                    for h in range(HG):
                        lhs = v_nat[:, j, g] if k == "values" else ones[:, 0:D]
                        last = nc.tensor.matmul(acc[D * h:D * h + D, 0 if k == "values" else 1, off:], lhs,
                                                probs[:, slot % 2, h, off:], start=first, stop=end)
                    if k == "sums":
                        last.then_inc(probs_used, 1)
                if k == "epilogue":
                    pe.wait_ge(probs_used, pv_index[(a[0], a[1], a[2], TPC * (a[0] + 1) - 1)] + 1)
                    pe.nop().then_inc(acc_full, 1)


_INS = ["L0_attn_x", "L0_attn_Wq", "L0_attn_Wk", "L0_attn_Wv", "L0_attn_Wo", "L0_attn_head_scales", "L0_ffn_W_syn",
        "L0_ffn_b_syn", "L0_ffn_W_out", "L0_ffn_b_out", "L0_ffn_gamma", "L0_ffn_beta"]
_OUTS = [((1, T, C), "float32")]


def shape_tables():
    import numpy as np
    inv = np.float32(1.0) / np.float32(10000.0) ** (np.arange(0, D, 2, dtype=np.float32) / np.float32(D))
    f = np.arange(T, dtype=np.float32)[:, None] * inv[None, :].astype(np.float32)
    cos, sin = np.cos(f).astype(np.float32), np.sin(f).astype(np.float32)
    signs = np.array([[sx, sy, sz] for sx in (1.0, -1.0) for sy in (1.0, -1.0) for sz in (1.0, -1.0)], dtype=np.float32)
    return {"cos_table": np.concatenate([cos, cos], axis=1), "sin_table": np.concatenate([-sin, sin], axis=1),
            "dirs_table": (signs / np.sqrt(3.0)).astype(np.float32)}


def kernel(**inputs):
    import numpy as _np
    import concourse.bacc as _bacc
    from concourse import mybir as _mybir
    from concourse.bass_utils import run_bass_kernel_spmd as _run

    nc = _bacc.Bacc("TRN2", target_bir_lowering=False, num_devices=1)
    arrays, args = {}, []
    for name, a in [(n, inputs[n]) for n in _INS] + list(shape_tables().items()):
        a = _np.ascontiguousarray(a)
        arrays[f"in_{name}_dram"] = a
        args.append(nc.dram_tensor(f"in_{name}_dram", a.shape, _mybir.dt.from_np(a.dtype), kind="ExternalInput").ap())
    for i, (shape, dtype) in enumerate(_OUTS):
        dt = _mybir.dt.from_np(_np.dtype(dtype))
        args.append(nc.dram_tensor(f"out_{i}_dram", shape, dt, kind="ExternalOutput").ap())
    attention_and_ternary_ffn(nc, *args)
    r = _run(nc, [arrays], core_ids=[0])
    return r.results[0]["out_0_dram"]
```

```python
from contextlib import ExitStack

import concourse.bass as bass
from concourse import mybir

F32 = mybir.dt.float32
F32R = mybir.dt.float32r
ALU = mybir.AluOpType
ACT = mybir.ActivationFunctionType
AX = mybir.AxisListType

P = 128
T, C = 2048, 256
H, G, D = 8, 2, 32
HG = H // G
HALF = D // 2
CHUNK = 512
NCH = T // CHUNK
NT = T // P
TPC = CHUNK // P
KC = C // P
N = 1024
NN = N // P
KTOP = max(1, int(N * (1.0 - 0.9)))
TOP_ROUNDS = (KTOP + 7) // 8
RANKS = 16
FIRST_GUESS = 3.31
STEP_1, STEP_2 = 250, 400
EARLY = 260
AIM = KTOP - RANKS / 2 - 0.5
QKV = (H + 2 * G) * D
QK = (H + G) * D
STK = 3 * D
SROWS = STK + 2
GROWS = 5
BANKS = 3
SBUFS = 3
ATT_SCALE = float(D) ** -0.5
LN_EPS = 1e-5
HI_ROW = 64
MASKED = -1e30


def build_plan():
    def op(cols):
        return 75 + 1.04 * cols

    def side_units(item):
        k, a = item[0], item[1:]
        if k == "xT":
            return [(("xT",) + a, 150, "dve", op(C), True)]
        if k == "qkv":
            return [(("qkv",) + a, 1300, "dve", 3300, True)]
        if k == "stacks":
            return [(("qT", a[0], 0), 250, "act", 650, True), (("qT", a[0], 1), 250, "act", 650, True),
                    (("kT",) + a, 250, "dve", 2 * op(C), True)]
        if k == "max":
            t = a[0]
            return [(("S",) + a + (p,), 230, "dve", 50 + op(CHUNK if p < t // TPC else (t % TPC + 1) * P), False)
                    for p in range(t // TPC + 1)]
        if k == "mrow":
            return [(("mT",) + a, 250, "dve", 1300, True)]
        if k == "quant":
            return ([(("wsum",) + a, 100, "dve", 4500, True)]
                    + [(("wT", a[0], i), 250, "dve", op(CHUNK), True) for i in range(4)])
        if k == "up_xs":
            return [(("xsT",) + a, 150, "dve", 2 * op(C), False)]
        if k == "up_z":
            return [(("z", a[0], 0), 1100, "act", 700, True), (("z", a[0], 1), 1100, "act", 700, False)]
        if k == "keep":
            return [(("found",) + a, 60, "dve", 1600, False)]
        if k == "down_h":
            return [(("hT", a[0], 0), 250, "dve", 2 * op(CHUNK), True), (("hT", a[0], 1), 250, "dve", 2 * op(CHUNK), False)]
        if k == "down_o":
            return [(("fo",) + a, 1750, "dve", 1100, False)]
        if k == "oproj":
            return [(("o",) + a, 900, "dve", op(C), False)]
        return []

    alone = {"stats": 3500, "geo": 8500, "mx": 200, "weigh": 4600, "select": 8800}

    def up(t):
        return [("up_xs", t), ("up_z", t)]

    side = []
    for c in range(NCH):
        tiles = list(range(TPC * c, TPC * c + TPC))
        side += [("stats", c), ("xT", tiles[0]), ("qkv", tiles[0])]
        for t in tiles:
            side += [("xT", t + 1)] * (t + 1 in tiles) + [("stacks", t)] + [("qkv", t + 1)] * (t + 1 in tiles)
        for t in tiles:
            side += [("max", t, h) for h in range(H)] + [("mx", t)]
        side += [("mrow", c), ("chunk_ready", c), ("geo", c)]
    for m in range(2):
        side += [("weigh", m), ("quant", m)]
    side += up(0) + up(1)
    for t in range(NT + 2):
        side += [("select", t)] * (t < NT) + [("down_o", t - 2)] * (t > 1)
        if t > NT:
            break
        side += [("keep", t - 1)] * (t > 0) + [("up_xs", t + 2)] * (t + 2 < NT)
        side += [("down_h", t - 1)] * (t > 0) + [("up_z", t + 2)] * (t + 2 < NT)

    attention = []
    for c in range(NCH):
        for g in range(G):
            for kind in range(2):
                js = TPC * (c + 1)
                attention += [("score", c, g, kind, 0, h) for h in range(HG)]
                for j in range(js):
                    ahead = [("score", c, g, kind, j + 1, h) for h in range(HG)] if j + 1 < js else []
                    attention += ahead[:2] + [("values", c, g, kind, j)] + ahead[2:] + [("sums", c, g, kind, j)]
                attention += [("epilogue", c, g, kind)]
        attention += [("attended", c)]

    plan, units = [], {}
    now = {"pe": 0.0, "dve": 0.0, "act": 0.0}
    freed = [0.0] * BANKS
    exp_done, exp_of = [], {}
    ready, attended, geo_out = set(), set(), set()
    ai = si = 0
    signs = []
    pending, late = [], []
    while ai < len(attention) or si < len(side) or pending or late:
        blocked = si < len(side) and side[si][0] == "stats" and side[si][1] >= 2 and side[si][1] - 2 not in attended
        if not pending and not blocked and ((late and late[0][0] <= now["pe"]) or si < len(side) or (late and ai >= len(attention))):
            if late and (late[0][0] <= now["pe"] or si >= len(side)):
                item = late.pop(0)[1]
            else:
                item = side[si]
                si += 1
            if item[0] == "select":
                while signs and signs[0][1] <= item[1]:
                    plan.append(signs.pop(0))
                    now["act"] += 1700
                now["dve"] = max(now["dve"], now["act"])
            plan.append(item)
            if item[0] == "chunk_ready":
                ready.add(item[1])
            if item[0] == "geo":
                geo_out.add(item[1])
            if item[0] in alone:
                now["dve"] += alone[item[0]]
            pending = side_units(item)
            if not pending:
                continue
        can_attend = (ai < len(attention) and attention[ai][1] in ready
                      and not (attention[ai][0] == "score" and attention[ai][3] == 1 and attention[ai][1] not in geo_out))
        if pending:
            name, pe_ns, reader, ns, after = pending[0]
            n = len(units)
            at = max(freed[n % BANKS], now["dve"] if after else 0.0)
            if at <= now["pe"] + EARLY or not can_attend:
                units[name] = n
                plan.append(("unit",) + name)
                now["pe"] = max(now["pe"], at) + pe_ns
                now[reader] = max(now[reader], now["pe"] + 100) + ns
                if name[0] == "z" and name[2] == 1:
                    signs += [("sign", name[1], 0), ("sign", name[1], 1)]
                freed[n % BANKS] = now[reader]
                pending.pop(0)
                continue
        if not can_attend:
            continue
        item = attention[ai]
        ai += 1
        plan.append(item)
        if item[0] in ("score", "values", "sums"):
            c, j = item[1], item[4]
            share = 1 - max(0, j - TPC * c) / TPC
        if item[0] == "score":
            if len(exp_done) >= SBUFS:
                now["pe"] = max(now["pe"], exp_done[-SBUFS])
            now["pe"] += 215 * share + (60 if j >= TPC * c else 0)
            now["act"] = max(now["act"], now["pe"] + 100) + 427 * share
            exp_done.append(now["act"])
            if signs and item[5] == HG - 1:
                plan.append(signs.pop(0))
                now["act"] += 1700
            exp_of[item] = now["act"]
        if item[0] == "values":
            now["pe"] = max(now["pe"], exp_of[("score",) + item[1:] + (HG - 1,)] + 50)
        if item[0] in ("values", "sums"):
            now["pe"] += 1000 * share
        if item[0] == "epilogue":
            now["dve"] = max(now["dve"], now["pe"]) + 3000
        if item[0] == "attended":
            attended.add(item[1])
            late += [(now["pe"] + 12000, ("oproj", t)) for t in range(TPC * item[1], TPC * item[1] + TPC)]
    return plan, units


def attention_and_ternary_ffn(nc, x, Wq, Wk, Wv, Wo, head_scales, W_syn, b_syn, W_out, b_out, gamma, beta,
                              cos_table, sin_table, small_table, out):
    plan, unit = build_plan()
    order = {item: i for i, item in enumerate(plan)}
    ffn_last = {t: order[("unit", "fo", t)] > order[("unit", "o", t)] for t in range(NT)}
    score_index = {it: n for n, it in enumerate(i for i in plan if i[0] == "score")}
    pv_index = {it[1:]: n for n, it in enumerate(i for i in plan if i[0] == "sums")}
    epi_index = {it[1:]: n for n, it in enumerate(i for i in plan if i[0] == "epilogue")}
    oproj_index = {it[2]: n for n, it in enumerate(i for i in plan if i[:2] == ("unit", "o"))}

    ctx = ExitStack()
    with ctx:
        def sb(name, shape, dt=F32):
            return ctx.enter_context(nc.sbuf_tensor(name, shape, dt))

        def pb(name, shape):
            return ctx.enter_context(nc.psum_tensor(name, shape, F32))

        def sem(name):
            return ctx.enter_context(nc.semaphore(name))

        res = sb("res", [P, NT, C])
        xn = sb("xn", [P, NT, C])
        w_qkv = sb("w_qkv", [P, KC, QKV])
        w_o = sb("w_o", [P, G, C])
        tables = sb("tables", [P, 2, NT, D])
        cos, sin = tables[:, 0], tables[:, 1]
        small = sb("small", [P, H * 3 + RANKS])
        dirs = small[:, 0:H * 3].rearrange("p (h i) -> p h i", i=3)
        ranks = small[:, H * 3:]
        all_scales = sb("all_scales", [P, H])
        scale_h = sb("scale_h", [P, G])
        q_nat = sb("q_nat", [P, H, STK], F32R)
        k_nat = sb("k_nat", [P, G, STK], F32R)
        geo_prod = sb("geo_prod", [P, 2, H, 3])
        geo_nat = sb("geo_nat", [P, 2, H])
        q_stack = sb("q_stack", [SROWS, 2, H, CHUNK], F32R)
        k_stack = sb("k_stack", [SROWS, G, T], F32R)
        q_geo = sb("q_geo", [P, 2, G, CHUNK], F32R)
        k_geo = sb("k_geo", [P, G, T], F32R)
        head_rows = sb("head_rows", [P, 2, CHUNK])
        geo_row = head_rows[0:H]
        b_up = head_rows[HI_ROW:HI_ROW + 1].rearrange("p a n -> p (a n)")
        geo_split = sb("geo_split", [P, 2, CHUNK], F32R)
        geo_hi, geo_lo = geo_split[0:H], geo_split[32:32 + H]
        run_max = sb("run_max", [H, CHUNK])
        run_min = sb("run_min", [H, CHUNK])
        run_end = sb("run_end", [H, 2])
        maxima = sb("maxima", [96 + H, CHUNK], F32R)
        gm_hi, gm_lo, m_hi, m_lo = (maxima[32 * i:32 * i + H] for i in range(4))
        piece_max = sb("piece_max", [P, H, NCH])
        row_max = sb("row_max", [P, TPC, H])
        v_nat = sb("v_nat", [P, NT, G, D])
        ones = sb("ones", [P, P])
        probs = sb("probs", [P, 2, HG, CHUNK])
        o_raw = sb("o_raw", [P, CHUNK])
        d_raw = sb("d_raw", [P, CHUNK])
        mixed = sb("mixed", [P, G, CHUNK])
        minus_half = sb("minus_half", [P, TPC])
        ident = sb("ident", [P, P])
        ident_r = sb("ident_r", [P, P], F32R)
        xb = sb("xb", [P, C])
        mask = xb[:].rearrange("p (a n) -> p a n", a=2)
        mask_r = sb("mask_r", [P, 2, P], F32R)
        stats = sb("stats", [P, 6])
        mean_var = sb("mean_var", [P, TPC, 2])
        rstd = sb("rstd", [P, TPC])
        w_abs = sb("w_abs", [P, 1])
        w_scale = sb("w_scale", [P, 2])
        w_cut = sb("w_cut", [P, 2])
        up_T = sb("up_T", [P, KC, N], F32R)
        down_T = sb("down_T", [P, NN, C], F32R)
        b_up_r = sb("b_up_r", [HI_ROW + 1, N], F32R)
        ones_r = sb("ones_r", [HI_ROW + 1, P], F32R)
        b_down = sb("b_down", [P, C])
        gam = sb("gam", [P, C])
        bet = sb("bet", [P, C])
        xs_hi = sb("xs_hi", [P, KC, P], F32R)
        xs_lo = sb("xs_lo", [P, KC, P], F32R)
        z_work = sb("z_work", [P, 2, N])
        z, work = z_work[:, 0], z_work[:, 1]
        rot_a, rot_b = z[:, 0:QK], z[:, QK:2 * QK]
        qk = z[:, 2 * QK:3 * QK]
        xnT = work[:, 0:C].rearrange("p (k t) -> p k t", k=KC)
        z_buf = [z, tables[:].rearrange("p a t d -> p (a t d)"), head_rows[:].rearrange("p a n -> p (a n)")]
        junk = geo_split[:, 0].bitcast(mybir.dt.bfloat16)
        z_sum = sb("z_sum", [P, 3, 2])
        guess = sb("guess", [P, 3, 8])
        found = sb("found", [P, 3, 1])
        thresh = sb("thresh", [P, 3, 1])
        search = sb("search", [P, 4])
        top16 = sb("top16", [P, RANKS])
        onehot = sb("onehot", [P, RANKS])
        n_found = sb("n_found", [1, 1], mybir.dt.int32)
        w_raw = z_work[:].rearrange("p a n -> p (a n)")
        top8 = sb("top8", [P, TOP_ROUNDS, 8])
        h_split = sb("h_split", [P, 2, NN, P], F32R)
        h_hi, h_lo = h_split[:, 0], h_split[:, 1]
        w_neg = h_split[:].rearrange("p a n t -> p (a n t)")
        y = sb("y", [P, C])
        y_stats = sb("y_stats", [P, 6])
        y_mv = sb("y_mv", [P, 2])
        y_rstd = sb("y_rstd", [P, 1])

        side = pb("side", [P, BANKS, CHUNK])
        scores = pb("scores", [P, SBUFS, CHUNK])
        acc = pb("acc", [P, 2, CHUNK])

        x_in = [sem(f"x_in{c}") for c in range(NCH)]
        w_in = sem("w_in")
        late_in = sem("late_in")
        up_in = sem("up_in")
        down_in = sem("down_in")
        const_ready = sem("const_ready")
        pool_step = sem("pool_step")
        dve_step = sem("dve_step")
        side_full = sem("side_full")
        side_free = [sem(f"side_free{i}") for i in range(BANKS)]
        var_ready = sem("var_ready")
        rstd_ready = sem("rstd_ready")
        masks_ready = sem("masks_ready")
        xn_ready = sem("xn_ready")
        nat_ready = sem("nat_ready")
        mx_ready = sem("mx_ready")
        geo_ready = sem("geo_ready")
        geo_in = [sem(f"geo_in{c}") for c in range(NCH)]
        m_in = [sem(f"m_in{c}") for c in range(NCH)]
        m_low_in = [sem(f"m_low_in{c}") for c in range(NCH)]
        score_full = sem("score_full")
        probs_ready = sem("probs_ready")
        probs_used = sem("probs_used")
        acc_full = sem("acc_full")
        raw_ready = sem("raw_ready")
        raw_free = sem("raw_free")
        mixed_ready = sem("mixed_ready")
        quant_ready = sem("quant_ready")
        search_ready = sem("search_ready")
        hi_ready = sem("hi_ready")
        act_step = sem("act_step")
        fallback_step = sem("fallback_step")
        found_ready = sem("found_ready")
        hidden_ready = sem("hidden_ready")
        xb_ready = sem("xb_ready")
        y_ready = sem("y_ready")
        ffn_added = sem("ffn_added")
        stored = sem("stored")

        block = ctx.enter_context(nc.Block())

        def consumed(eng, n):
            eng.wait_ge(side_free[n % BANKS], n // BANKS + 1)

        x_rows = x.rearrange("o (c i p) d -> c p (o i) d", p=P, i=TPC)
        out_rows = out.rearrange("o (t p) d -> t p (o d)", p=P)
        N_W_IN = 16 * 6
        N_LATE_IN = 16 * 6
        N_FIRST_CONSTS = 7
        N_CONSTS = N_FIRST_CONSTS + 3

        @block.sync
        def _(sp):
            sp.dma_start(res[:, 0:TPC], x_rows[0]).then_inc(x_in[0], 16)
            for w, at in ((Wq, 0), (Wk, H * D), (Wv, QK)):
                sp.dma_start(w_qkv[:, :, at:at + w.shape[1]],
                             w.rearrange("(k p) n -> p k n", p=P)).then_inc(w_in, 16)
            sp.dma_start(cos, cos_table.rearrange("(t p) d -> p t d", p=P)).then_inc(w_in, 16)
            sp.dma_start(sin, sin_table.rearrange("(t p) d -> p t d", p=P)).then_inc(w_in, 16)
            sp.dma_start(small[:], small_table.broadcast_to([P, H * 3 + RANKS])).then_inc(w_in, 16)
            for c in range(1, NCH):
                sp.dma_start(res[:, TPC * c:TPC * c + TPC], x_rows[c]).then_inc(x_in[c], 16)
            sp.dma_start(w_o[:], Wo.rearrange("(g p) n -> p g n", p=P)).then_inc(late_in, 16)
            for t_, v_ in ((all_scales, head_scales), (b_down, b_out), (gam, gamma), (bet, beta)):
                sp.dma_start(t_[:], v_.rearrange("(o n) -> o n", o=1).broadcast_to([P, v_.shape[0]])).then_inc(late_in, 16)
            sp.dma_start(b_up, b_syn.rearrange("(o n) -> o n", o=1)).then_inc(late_in, 16)
            for item in plan:
                k = item[0]
                if k == "geo":
                    c = item[1]
                    b, cols = c % 2, slice(CHUNK * c, CHUNK * c + CHUNK)
                    sp.wait_ge(geo_ready, c + 1)
                    if c == 0:
                        sp.wait_ge(const_ready, N_CONSTS)
                    if c >= 2:
                        sp.wait_ge(acc_full, 2 * G * (c - 1))
                    for g in range(G):
                        hs_ = slice(HG * g, HG * g + HG)
                        for r, src in enumerate((geo_hi[hs_, 0], geo_lo[hs_, 0], geo_hi[hs_, 0])):
                            sp.dma_start(k_geo[r:r + 97:32, g, cols].bitcast(F32), src.bitcast(F32)).then_inc(geo_in[c], 16)
                        for r, src in enumerate((geo_hi[hs_, 1], geo_hi[hs_, 1], geo_lo[hs_, 1],
                                                 gm_hi[hs_], gm_lo[hs_])):
                            sp.dma_start(q_geo[r:r + 97:32, b, g, :].bitcast(F32), src.bitcast(F32)).then_inc(geo_in[c], 16)
                if k == "chunk_ready":
                    c = item[1]
                    consumed(sp, unit[("mT", c)])
                    sp.dma_start(q_stack[STK:STK + 1, c % 2].bitcast(F32),
                                 m_hi.bitcast(F32)).then_inc(m_in[c], 16)
                if item == ("weigh", 0):
                    sp.wait_ge(nat_ready, NT)
                    sp.dma_start(w_raw.rearrange("p (a n) -> p a n", a=NN),
                                 W_syn.rearrange("(a p) n -> p a n", p=P)).then_inc(up_in, 16)
                if item == ("weigh", 1):
                    consumed(sp, unit[("wT", 0, 3)])
                    sp.dma_start(w_raw.rearrange("p (a n) -> p a n", a=KC),
                                 W_out.rearrange("(a p) n -> p a n", p=P)).then_inc(down_in, 16)
                if k == "unit" and item[1] in ("o", "fo"):
                    t = item[2]
                    if ffn_last[t] == (item[1] == "fo"):
                        if ffn_last[t]:
                            sp.wait_ge(ffn_added, t + 1)
                        else:
                            consumed(sp, unit[("o", t)])
                        sp.dma_start(out_rows[t], res[:, t]).then_inc(stored, 16)
            sp.wait_ge(stored, 16 * NT)

        @block.gpsimd
        def _(pool):
            steps = [0]

            def link(ins):
                steps[0] += 1
                ins.then_inc(pool_step, 1)
                pool.wait_ge(pool_step, steps[0])

            consts = [0]

            def constant(ins):
                consts[0] += 1
                ins.then_inc(const_ready, 1)
                pool.wait_ge(const_ready, consts[0])

            constant(nc.gpsimd.memset(ident[:], 0.0))
            constant(nc.gpsimd.affine_select(out=ident[:], in_=ident[:], compare_op=ALU.not_equal, fill=1.0, base=0,
                                             pattern=[[-1, P]], channel_multiplier=1))
            constant(nc.gpsimd.memset(minus_half[:], -0.5))
            constant(nc.gpsimd.memset(ones[:], 1.0))
            constant(nc.gpsimd.memset(xb[:], 0.0))
            constant(nc.gpsimd.affine_select(out=mask[:, 0], in_=mask[:, 0], compare_op=ALU.is_ge, fill=MASKED, base=0,
                                             pattern=[[1, P]], channel_multiplier=-1))
            constant(nc.gpsimd.affine_select(out=mask[:, 1], in_=mask[:, 1], compare_op=ALU.is_ge, fill=MASKED, base=0,
                                             pattern=[[-1, P]], channel_multiplier=1))

            def late_constants():
                for ap, value in ((k_stack[STK:SROWS], -1.0), (k_geo[:], -1.0), (b_up_r[:], 0.0)):
                    constant(nc.gpsimd.memset(ap.bitcast(F32), value))

            for item in plan:
                k = item[0]
                if k == "stats":
                    pool.wait_ge(var_ready, item[1] + 1)
                    nc.gpsimd.tensor_tensor(rstd[:], mean_var[:, :, 1], minus_half[:], ALU.pow).then_inc(rstd_ready, 1)
                    if item[1] == 0:
                        pool.wait_ge(rstd_ready, 1)
                        late_constants()
                if k == "chunk_ready":
                    c = item[1]
                    consumed(pool, unit[("mT", c)])
                    pool.dma_start(q_stack[STK + 1:STK + 2, c % 2].bitcast(F32),
                                   m_lo.bitcast(F32)).then_inc(m_low_in[c], 16)
                if k == "epilogue":
                    c, g, kind = item[1:]
                    n = epi_index[item[1:]]
                    pool.wait_ge(raw_ready, 2 * (n + 1))
                    if n == 0:
                        pool.wait_ge(late_in, N_LATE_IN)
                        for h in range(HG):
                            rows = slice(D * h, D * h + D)
                            link(nc.gpsimd.tensor_copy(scale_h[rows, :], all_scales[rows].rearrange(
                                "p (g h) -> p g h", g=G)[:, :, h]))
                    if kind == 0:
                        if c >= 1:
                            pool.wait_ge(side_full, unit[("o", TPC * c - 1)] + 1)
                        nc.gpsimd.tensor_tensor(mixed[:, g], o_raw[:], d_raw[:], ALU.mult).then_inc(raw_free, 1)
                        pool.wait_ge(raw_free, n + 1)
                    else:
                        link(nc.gpsimd.tensor_tensor(o_raw[:], o_raw[:], d_raw[:], ALU.mult))
                        link(nc.gpsimd.tensor_tensor(o_raw[:], o_raw[:], mixed[:, g], ALU.subtract))
                        link(nc.gpsimd.tensor_scalar(o_raw[:], o_raw[:], scale_h[:, g:g + 1], None, ALU.mult))
                        link(nc.gpsimd.tensor_tensor(mixed[:, g], o_raw[:], mixed[:, g], ALU.add))
                        pool.nop().then_inc(raw_free, 1)
                        pool.nop().then_inc(mixed_ready, 1)
                if k == "down_h":
                    t = item[1]
                    if t >= 1:
                        pool.wait_ge(y_ready, t)
                    nc.gpsimd.tensor_tensor(xb[:], xn[:, t], b_down[:], ALU.add).then_inc(xb_ready, 1)
                if k == "unit" and item[1] == "fo":
                    t = item[2]
                    pool.wait_ge(y_ready, t + 1)
                    link(nc.gpsimd.tensor_tensor(y_rstd[:], y_mv[:, 1:2], minus_half[:, 0:1], ALU.pow))
                    link(nc.gpsimd.tensor_scalar(y[:], y[:], y_mv[:, 0:1], y_rstd[:, 0:1], ALU.subtract, ALU.mult))
                    link(nc.gpsimd.tensor_tensor(y[:], y[:], gam[:], ALU.mult))
                    link(nc.gpsimd.tensor_tensor(y[:], y[:], bet[:], ALU.add))
                    if ffn_last[t]:
                        consumed(pool, unit[("o", t)])
                    nc.gpsimd.tensor_tensor(res[:, t], res[:, t], y[:], ALU.add).then_inc(ffn_added, 1)

        @block.scalar
        def _(act):
            steps = [0]

            def link(ins):
                steps[0] += 1
                ins.then_inc(act_step, 1)
                act.wait_ge(act_step, steps[0])

            for item in plan:
                k, a = item[0], item[1:]
                if k == "score":
                    c, g, kind, j, h = a
                    n = score_index[item]
                    off = max(0, j - TPC * c) * P
                    slot = pv_index[(c, g, kind, j)]
                    act.wait_ge(score_full, n + 1)
                    if h == 0 and slot >= 2:
                        act.wait_ge(probs_used, slot - 1)
                    nc.scalar.activation(probs[:, slot % 2, h, off:], scores[:, n % SBUFS, off:], ACT.Exp,
                                         scale=ATT_SCALE if kind == 0 else 1.0).then_inc(probs_ready, 1)
                if k == "unit" and a[0] == "qT":
                    t, half = a[1:]
                    c, col = t // TPC, t % TPC * P
                    act.wait_ge(side_full, unit[a] + 1)
                    if half == 0 and t % TPC == 0 and c >= 2:
                        act.wait_ge(acc_full, 2 * G * (c - 1))
                    nc.scalar.copy(q_stack[0:STK, c % 2, 4 * half:4 * half + 4, col:col + P],
                                   side[0:STK, unit[a] % BANKS].rearrange("p (h t) -> p h t", t=P)
                                   ).then_inc(side_free[unit[a] % BANKS], 1)
                if k == "unit" and a[0] == "z":
                    t, half = a[1:]
                    zt = z_buf[t % 3]
                    act.wait_ge(side_full, unit[a] + 1)
                    if half == 0:
                        if t >= 3:
                            act.wait_ge(hidden_ready, t - 2)
                        if t == 0:
                            consumed(act, unit[("wT", 1, 3)])
                    nc.scalar.activation(zt[:, CHUNK * half:CHUNK * half + CHUNK], side[:, unit[a] % BANKS], ACT.Relu,
                                         accum_out=z_sum[:, t % 3, half:half + 1]).then_inc(side_free[unit[a] % BANKS], 1)
                if k == "unit" and a[0] == "hT":
                    t, half = a[1:]
                    act.wait_ge(side_full, unit[a] + 1)
                    nc.scalar.copy(h_hi[:, 4 * half:4 * half + 4],
                                   side[:, unit[a] % BANKS].rearrange("p (a t) -> p a t", t=P)).then_inc(hi_ready, 1)
                if k == "sign":
                    t, i = a
                    zt, q = z_buf[t % 3], guess[:, t % 3]
                    if i == 0:
                        for b in range(2):
                            consumed(act, unit[("z", t, b)])
                        link(nc.scalar.mul(q[:, 0:1], z_sum[:, t % 3, 0:1], -FIRST_GUESS / N))
                        link(nc.scalar.activation(q[:, 1:2], z_sum[:, t % 3, 1:2], ACT.Identity, bias=q[:, 0:1],
                                                  scale=-FIRST_GUESS / N))
                        link(nc.scalar.activation(junk, zt, ACT.Sign, bias=q[:, 1:2], accum_out=q[:, 2:3]))
                    else:
                        link(nc.scalar.activation(q[:, 3:4], q[:, 2:3], ACT.Copy, scale=0.5 / STEP_1,
                                                  bias=1 + (N / 2 - AIM) / STEP_1))
                        link(nc.scalar.activation(q[:, 4:5], q[:, 1:2], ACT.Copy, scale=q[:, 3:4]))
                        nc.scalar.activation(junk, zt, ACT.Sign, bias=q[:, 4:5],
                                             accum_out=q[:, 5:6]).then_inc(search_ready, 1)
                        act.wait_ge(search_ready, t + 1)

        @block.vector
        def _(dve):
            steps = [0]

            def mark(ins):
                steps[0] += 1
                ins.then_inc(dve_step, 1)

            def settle():
                dve.wait_ge(dve_step, steps[0])

            def link(ins):
                mark(ins)
                settle()

            def filled(name):
                dve.wait_ge(side_full, unit[name] + 1)
                return side[:, unit[name] % BANKS]

            def free(ins, name):
                ins.then_inc(side_free[unit[name] % BANKS], 1)

            def row_stats(c):
                dve.wait_ge(x_in[c], 16)
                for i in range(TPC):
                    link(nc.vector.bn_stats(stats[:], res[:, TPC * c + i]))
                    link(nc.vector.bn_aggr(mean_var[:, i, :], stats[:]))
                nc.vector.tensor_scalar(mean_var[:, :, 1], mean_var[:, :, 1], LN_EPS, None, ALU.add).then_inc(var_ready, 1)
                dve.wait_ge(rstd_ready, c + 1)
                for i in range(TPC):
                    nc.vector.tensor_scalar(xn[:, TPC * c + i], res[:, TPC * c + i], mean_var[:, i, 0:1],
                                            rstd[:, i:i + 1], ALU.subtract, ALU.mult).then_inc(xn_ready, 1)

            row_stats(0)
            dve.wait_ge(const_ready, N_FIRST_CONSTS)
            link(nc.vector.tensor_copy(ident_r[:], ident[:]))
            mark(nc.vector.tensor_copy(ones_r[:], ones[0:HI_ROW + 1, :]))
            mark(nc.vector.memset(run_end[:, 0:1], -3.0e38))
            mark(nc.vector.memset(run_end[:, 1:2], 3.0e38))
            nc.vector.tensor_copy(mask_r[:], mask).then_inc(masks_ready, 1)
            dve.wait_ge(masks_ready, 1)
            settle()

            for item in plan:
                k, a = item[0], item[1:]
                if k == "stats" and a[0] > 0:
                    row_stats(a[0])
                if k == "unit" and a[0] == "xT":
                    pt = filled(a)
                    free(nc.vector.tensor_copy(xnT, pt[:, 0:C].rearrange("p (k t) -> p k t", k=KC)), a)
                if k == "unit" and a[0] == "qkv":
                    t = a[1]
                    if t == 0:
                        dve.wait_ge(w_in, N_W_IN)
                    pt = filled(a)
                    pq = pt[:, 0:QK].rearrange("p (h f i) -> p h f i", f=2, i=HALF)
                    rb = rot_b.rearrange("p (h f i) -> p h f i", f=2, i=HALF)
                    mark(nc.vector.tensor_tensor(rot_a.rearrange("p (h d) -> p h d", d=D),
                                                 pt[:, 0:QK].rearrange("p (h d) -> p h d", d=D),
                                                 cos[:, t:t + 1, :].broadcast_to([P, H + G, D]), ALU.mult))
                    for f in range(2):
                        mark(nc.vector.tensor_tensor(
                            rb[:, :, f], pq[:, :, 1 - f],
                            sin[:, t:t + 1, HALF * f:HALF * f + HALF].broadcast_to([P, H + G, HALF]), ALU.mult))
                    mark(nc.vector.tensor_copy(v_nat[:, t], pt[:, QK:QKV].rearrange("p (g d) -> p g d", g=G)))
                    settle()
                    nc.vector.tensor_tensor(qk, rot_a, rot_b, ALU.add).then_inc(side_free[unit[a] % BANKS], 1)
                    consumed(dve, unit[a])
                    q = qk[:, 0:H * D].rearrange("p (h d) -> p h d", d=D)
                    kk = qk[:, H * D:QK].rearrange("p (g d) -> p g d", d=D)
                    mark(nc.vector.tensor_copy(q_nat[:, :, 0:D], q))
                    mark(nc.vector.tensor_copy(q_nat[:, :, D:2 * D], q))
                    mark(nc.vector.tensor_copy(k_nat[:, :, 0:D], kk))
                    mark(nc.vector.tensor_copy(k_nat[:, :, 2 * D:], kk))
                    mark(nc.vector.tensor_tensor(geo_prod[:, 1], q[:, :, 0:3], dirs, ALU.mult))
                    for g in range(G):
                        hs_ = slice(HG * g, HG * g + HG)
                        mark(nc.vector.tensor_tensor(geo_prod[:, 0, hs_], kk[:, g:g + 1, 0:3].broadcast_to([P, HG, 3]),
                                                     dirs[:, hs_], ALU.mult))
                    settle()
                    mark(nc.vector.tensor_tensor(q_nat[:, :, 2 * D:], q, q_nat[:, :, 0:D].bitcast(F32), ALU.subtract))
                    mark(nc.vector.tensor_tensor(k_nat[:, :, D:2 * D], kk, k_nat[:, :, 0:D].bitcast(F32), ALU.subtract))
                    nc.vector.tensor_reduce(geo_nat[:], geo_prod[:], AX.X, ALU.add).then_inc(nat_ready, 1)
                    settle()
                    dve.wait_ge(nat_ready, t + 1)
                if k == "unit" and a[0] == "kT":
                    t = a[1]
                    col = t % TPC * P
                    pt = filled(a)
                    mark(nc.vector.tensor_copy(k_stack[0:STK, :, P * t:P * t + P],
                                               pt[0:STK, 0:G * P].rearrange("p (g t) -> p g t", t=P)))
                    free(nc.vector.tensor_copy(geo_row[:, :, col:col + P],
                                               pt[0:H, G * P:G * P + 2 * P].rearrange("p (a t) -> p a t", t=P)), a)
                    settle()
                    consumed(dve, unit[a])
                if k == "geo":
                    c = a[0]
                    kp, qp = geo_row[:, 0], geo_row[:, 1]
                    if c >= 1:
                        dve.wait_ge(geo_in[c - 1], 16 * 8 * G)
                    mark(nc.vector.tensor_copy(geo_hi, geo_row))
                    mark(nc.vector.tensor_tensor_scan(run_max[:], kp, kp, run_end[:, 0:1], ALU.max, ALU.max))
                    mark(nc.vector.tensor_tensor_scan(run_min[:], kp, kp, run_end[:, 1:2], ALU.min, ALU.min))
                    settle()
                    mark(nc.vector.tensor_tensor(geo_lo, geo_row, geo_hi.bitcast(F32), ALU.subtract))
                    mark(nc.vector.tensor_copy(run_end[:, 0:1], run_max[:, CHUNK - 1:]))
                    mark(nc.vector.tensor_copy(run_end[:, 1:2], run_min[:, CHUNK - 1:]))
                    settle()
                    mark(nc.vector.tensor_tensor(run_max[:], run_max[:], qp, ALU.mult))
                    mark(nc.vector.tensor_tensor(run_min[:], run_min[:], qp, ALU.mult))
                    settle()
                    link(nc.vector.tensor_tensor(run_max[:], run_max[:], run_min[:], ALU.max))
                    link(nc.vector.tensor_copy(gm_hi, run_max[:]))
                    nc.vector.tensor_tensor(gm_lo, run_max[:], gm_hi.bitcast(F32), ALU.subtract).then_inc(geo_ready, 1)
                    dve.wait_ge(geo_ready, c + 1)
                if k == "unit" and a[0] == "S":
                    t, h, p = a[1:]
                    ncol = CHUNK if p < t // TPC else (t % TPC + 1) * P
                    pt = filled(a)
                    free(nc.vector.tensor_reduce(piece_max[:, h, p:p + 1], pt[:, 0:ncol], AX.X, ALU.max), a)
                if k == "mx":
                    t = a[0]
                    for back in range(BANKS):
                        consumed(dve, unit[("S", t, H - 1, t // TPC)] - back)
                    if t % TPC == 0 and t >= TPC:
                        dve.wait_ge(side_full, unit[("mT", t // TPC - 1)] + 1)
                    ins = nc.vector.tensor_reduce(row_max[:, t % TPC], piece_max[:, :, 0:t // TPC + 1], AX.X, ALU.max)
                    ins.then_inc(mx_ready, 1)
                    dve.wait_ge(mx_ready, t + 1)
                if k == "unit" and a[0] == "mT":
                    c = a[1]
                    pt = filled(a)
                    if c >= 1:
                        dve.wait_ge(m_in[c - 1], 16)
                        dve.wait_ge(m_low_in[c - 1], 16)
                    link(nc.vector.tensor_copy(m_hi, pt[0:H]))
                    free(nc.vector.tensor_tensor(m_lo, pt[0:H], m_hi.bitcast(F32), ALU.subtract), a)
                if k == "epilogue":
                    n = epi_index[a]
                    dve.wait_ge(acc_full, n + 1)
                    if n >= 1:
                        dve.wait_ge(raw_free, n)
                    nc.vector.tensor_copy(o_raw[:], acc[:, 0]).then_inc(raw_ready, 1)
                    nc.vector.reciprocal(d_raw[:], acc[:, 1]).then_inc(raw_ready, 1)
                if k == "unit" and a[0] == "o":
                    t = a[1]
                    pt = filled(a)
                    if not ffn_last[t]:
                        dve.wait_ge(ffn_added, t + 1)
                    free(nc.vector.tensor_tensor(res[:, t], pt[:, 0:C], res[:, t], ALU.add), a)
                if k == "weigh":
                    m = a[0]
                    dve.wait_ge(up_in if m == 0 else down_in, 16)
                    if m == 1:
                        consumed(dve, unit[("wT", 0, 3)])
                    nc.vector.tensor_reduce(w_abs[:], w_raw, AX.X, ALU.add,
                                            apply_absolute_value=True).then_inc(quant_ready, 1)
                if k == "unit" and a[0] == "wsum":
                    m = a[1]
                    pt = filled(a)
                    link(nc.vector.tensor_scalar(w_scale[:, m:m + 1], pt[:, 0:1], 1.0 / (N * C), None, ALU.mult))
                    link(nc.vector.tensor_scalar(w_cut[:, 0:1], w_scale[:, m:m + 1], 1e-8, 0.5, ALU.add, ALU.mult))
                    link(nc.vector.tensor_scalar(w_cut[:, 1:2], w_cut[:, 0:1], -1.0, None, ALU.mult))
                    link(nc.vector.tensor_scalar(w_neg, w_raw, w_cut[:, 1:2], None, ALU.is_lt))
                    free(nc.vector.scalar_tensor_tensor(w_neg, w_raw, w_cut[:, 0:1], w_neg.bitcast(F32), ALU.is_gt,
                                                        ALU.subtract), a)
                if k == "unit" and a[0] == "wT":
                    m, i = a[1:]
                    pt = filled(a)
                    if m == 0:
                        dst = up_T[:, i // 2, CHUNK * (i % 2):CHUNK * (i % 2) + CHUNK]
                        src = pt
                    else:
                        dst = down_T[:, 2 * i:2 * i + 2, :]
                        src = pt.rearrange("p (a n) -> p a n", a=2)
                    free(nc.vector.tensor_copy(dst, src), a)
                    if m == 0 and i == 3:
                        dve.wait_ge(late_in, N_LATE_IN)
                        dve.wait_ge(const_ready, N_CONSTS)
                        link(nc.vector.tensor_copy(b_up_r[HI_ROW:HI_ROW + 1, :], b_up))
                        link(nc.vector.tensor_tensor(b_up_r[0:1, :], b_up, b_up_r[HI_ROW:HI_ROW + 1, :].bitcast(F32), ALU.subtract))
                if k == "unit" and a[0] == "xsT":
                    t = a[1]
                    pt = filled(a)
                    pt3 = pt[:, 0:C].rearrange("p (k t) -> p k t", k=KC)
                    link(nc.vector.tensor_scalar(xs_hi[:], pt3, w_scale[:, 0:1], None, ALU.mult))
                    free(nc.vector.scalar_tensor_tensor(xs_lo[:], pt3, w_scale[:, 0:1], xs_hi[:].bitcast(F32), ALU.mult,
                                                        ALU.subtract), a)
                if k == "select":
                    t = a[0]
                    zt, q = z_buf[t % 3], guess[:, t % 3]
                    dve.wait_ge(search_ready, t + 1)
                    link(nc.vector.tensor_scalar(search[:, 0:1], q[:, 5:6], 0.5 / STEP_2,
                                                 1 + (N / 2 - AIM) / STEP_2, ALU.mult, ALU.add))
                    link(nc.vector.tensor_scalar(search[:, 1:2], search[:, 0:1], q[:, 4:5], -1.0, ALU.mult, ALU.mult))
                    link(nc.vector.tensor_scalar(work, zt, search[:, 1:2], None, ALU.is_ge, ALU.add,
                                                 accum_out=search[:, 2:3]))
                    mark(nc.vector.tensor_scalar(search[:, 3:4], search[:, 2:3], -1.0, float(KTOP), ALU.mult, ALU.add))
                    link(nc.vector.scalar_tensor_tensor(work, zt, search[:, 1:2], zt, ALU.is_lt, ALU.mult))
                    link(nc.vector.max(top16[:, 0:8], work))
                    link(nc.vector.match_replace(work, top16[:, 0:8], work, -1.0))
                    mark(nc.vector.max(top16[:, 8:16], work))
                    nc.vector.tensor_scalar(onehot[:], ranks, search[:, 3:4], None, ALU.is_equal, ALU.add,
                                            accum_out=found[:, t % 3]).then_inc(found_ready, 1)
                    dve.wait_ge(found_ready, t + 1)
                    link(nc.vector.scalar_tensor_tensor(onehot[:], ranks, search[:, 3:4], top16[:], ALU.is_equal, ALU.mult,
                                                        accum_out=thresh[:, t % 3]))
                if k == "unit" and a[0] == "found":
                    t = a[1]
                    zt = z_buf[t % 3]
                    free(nc.vector.tensor_copy(n_found[:], filled(a)[0:1, 0:1]), a)
                    consumed(dve, unit[a])
                    rows_found = dve.value_load(n_found[0:1, 0:1], min_val=0, max_val=P)
                    before = (2 * TOP_ROUNDS) * t
                    with dve.If(rows_found < P):
                        cur = zt
                        for r in range(TOP_ROUNDS):
                            nc.vector.max(top8[:, r], cur).then_inc(fallback_step, 1)
                            dve.wait_ge(fallback_step, before + 2 * r + 1)
                            if r < TOP_ROUNDS - 1:
                                nc.vector.match_replace(work, top8[:, r], cur, -1.0).then_inc(fallback_step, 1)
                                dve.wait_ge(fallback_step, before + 2 * r + 2)
                            cur = work
                        last = (KTOP - 1) % 8
                        nc.vector.tensor_copy(thresh[:, t % 3], top8[:, TOP_ROUNDS - 1, last:last + 1]
                                              ).then_inc(fallback_step, 1)
                    with dve.Else():
                        dve.sem_inc(fallback_step, 2 * TOP_ROUNDS)
                    dve.wait_ge(fallback_step, before + 2 * TOP_ROUNDS)
                    nc.vector.scalar_tensor_tensor(work, zt, thresh[:, t % 3], zt, ALU.is_ge,
                                                   ALU.mult).then_inc(hidden_ready, 1)
                    dve.wait_ge(hidden_ready, t + 1)
                if k == "unit" and a[0] == "hT":
                    t, half = a[1:]
                    pt = filled(a).rearrange("p (a t) -> p a t", t=P)
                    s_ = slice(4 * half, 4 * half + 4)
                    dve.wait_ge(hi_ready, 2 * t + half + 1)
                    free(nc.vector.tensor_tensor(h_lo[:, s_], pt, h_hi[:, s_].bitcast(F32), ALU.subtract), a)
                if k == "unit" and a[0] == "fo":
                    t = a[1]
                    pt = filled(a)
                    dve.wait_ge(xb_ready, t + 1)
                    if t >= 1:
                        dve.wait_ge(ffn_added, t)
                    link(nc.vector.scalar_tensor_tensor(y[:], pt[:, 0:C], w_scale[:, 1:2], xb[:], ALU.mult, ALU.add))
                    free(nc.vector.bn_stats(y_stats[:], y[:]), a)
                    consumed(dve, unit[a])
                    link(nc.vector.bn_aggr(y_mv[:], y_stats[:]))
                    nc.vector.tensor_scalar(y_mv[:, 1:2], y_mv[:, 1:2], LN_EPS, None, ALU.add).then_inc(y_ready, 1)
                    dve.wait_ge(y_ready, t + 1)

        @block.tensor
        def _(pe):
            pe.wait_ge(const_ready, N_FIRST_CONSTS)
            pe.wait_ge(masks_ready, 1)
            for item in plan:
                k, a = item[0], item[1:]
                if k == "unit":
                    n = unit[a]
                    pt = side[:, n % BANKS]
                    if n >= BANKS:
                        consumed(pe, n - BANKS)
                    if a[0] == "xT":
                        t = a[1]
                        pe.wait_ge(xn_ready, t + 1)
                        for i in range(KC):
                            last = nc.tensor.transpose(pt[:, P * i:P * i + P], xn[:, t, P * i:P * i + P], ident[:])
                    if a[0] == "qkv":
                        t = a[1]
                        consumed(pe, unit[("xT", t)])
                        if t == 0:
                            pe.wait_ge(w_in, N_W_IN)
                        for i in range(KC):
                            last = nc.tensor.matmul(pt[:, 0:QKV], xnT[:, i], w_qkv[:, i], start=(i == 0), stop=(i == KC - 1))
                    if a[0] == "qT":
                        t, half = a[1:]
                        pe.wait_ge(nat_ready, t + 1)
                        for i in range(4):
                            last = nc.tensor.transpose(pt[0:STK, P * i:P * i + P], q_nat[:, 4 * half + i].bitcast(F32), ident[:])
                    if a[0] == "kT":
                        t = a[1]
                        for g in range(G):
                            nc.tensor.transpose(pt[0:STK, P * g:P * g + P], k_nat[:, g].bitcast(F32), ident[:])
                        for i in range(2):
                            last = nc.tensor.transpose(pt[0:H, P * (G + i):P * (G + i) + P], geo_nat[:, i], ident[:])
                    if a[0] == "S":
                        t, h, p = a[1:]
                        c, b, col = t // TPC, t // TPC % 2, t % TPC * P
                        if h == 0 and p == 0:
                            for back in range(BANKS):
                                consumed(pe, unit[("kT", TPC * c + TPC - 1)] - back)
                        full = p < c
                        ncol = CHUNK if full else col + P
                        last = nc.tensor.matmul(pt[:, 0:ncol], q_stack[0:STK, b, h, col:col + P],
                                                k_stack[0:STK, h // HG, CHUNK * p:CHUNK * p + ncol], start=True, stop=full)
                        if not full:
                            last = nc.tensor.matmul(pt[:, col:col + P], ident_r[:], mask_r[:, 1], start=False, stop=True)
                    if a[0] == "mT":
                        c = a[1]
                        pe.wait_ge(mx_ready, TPC * (c + 1))
                        for i in range(TPC):
                            last = nc.tensor.transpose(pt[0:H, P * i:P * i + P], row_max[:, i], ident[:])
                    if a[0] == "wsum":
                        pe.wait_ge(quant_ready, a[1] + 1)
                        last = nc.tensor.matmul(pt[:, 0:1], ones[:], w_abs[:], start=True, stop=True)
                    if a[0] == "found":
                        pe.wait_ge(found_ready, a[1] + 1)
                        last = nc.tensor.matmul(pt[0:1, 0:1], found[:, a[1] % 3], ones[:, 0:1], start=True, stop=True)
                    if a[0] == "wT":
                        m, i = a[1:]
                        consumed(pe, unit[("wsum", m)])
                        for q in range(4):
                            if m == 0:
                                nt = 4 * (i % 2) + q
                                at = nt * C + (i // 2) * P
                            else:
                                nt, dt_ = 2 * i + q // 2, q % 2
                                at = dt_ * N + nt * P
                            last = nc.tensor.transpose(pt[:, P * q:P * q + P], w_neg[:, at:at + P].bitcast(F32), ident[:])
                    if a[0] == "xsT":
                        t = a[1]
                        for i in range(KC):
                            last = nc.tensor.transpose(pt[:, P * i:P * i + P], xn[:, t, P * i:P * i + P], ident[:])
                    if a[0] == "z":
                        t, half = a[1:]
                        consumed(pe, unit[("xsT", t)])
                        cols = slice(CHUNK * half, CHUNK * half + CHUNK)
                        for i in range(KC):
                            nc.tensor.matmul(pt, xs_hi[:, i], up_T[:, i, cols], start=(i == 0), stop=False)
                            nc.tensor.matmul(pt, xs_lo[:, i], up_T[:, i, cols], start=False, stop=False)
                        last = nc.tensor.matmul(pt, ones_r[:], b_up_r[:, cols], start=False, stop=True)
                    if a[0] == "hT":
                        t, half = a[1:]
                        pe.wait_ge(hidden_ready, t + 1)
                        for i in range(4):
                            at = P * (4 * half + i)
                            last = nc.tensor.transpose(pt[:, P * i:P * i + P], work[:, at:at + P], ident[:])
                    if a[0] == "fo":
                        t = a[1]
                        for half in range(2):
                            consumed(pe, unit[("hT", t, half)])
                        for i in range(NN):
                            nc.tensor.matmul(pt[:, 0:C], h_hi[:, i], down_T[:, i], start=(i == 0), stop=False)
                            last = nc.tensor.matmul(pt[:, 0:C], h_lo[:, i], down_T[:, i], start=False, stop=(i == NN - 1))
                    if a[0] == "o":
                        t = a[1]
                        c, col = t // TPC, t % TPC * P
                        pe.wait_ge(mixed_ready, G * (c + 1))
                        pe.wait_ge(late_in, N_LATE_IN)
                        for g in range(G):
                            last = nc.tensor.matmul(pt[:, 0:C], mixed[:, g, col:col + P], w_o[:, g], start=(g == 0), stop=(g == G - 1))
                    last.then_inc(side_full, 1)
                if k == "score":
                    c, g, kind, j, h = a
                    n = score_index[item]
                    b = c % 2
                    off = max(0, j - TPC * c) * P
                    if n == 0:
                        pe.wait_ge(const_ready, N_CONSTS)
                    if n >= SBUFS:
                        pe.wait_ge(probs_ready, n - SBUFS + 1)
                    if g == 0 and j == 0 and h == 0:
                        if kind == 0:
                            pe.wait_ge(m_in[c], 16)
                            pe.wait_ge(m_low_in[c], 16)
                        else:
                            pe.wait_ge(geo_in[c], 16 * 8 * G)
                    diagonal = j >= TPC * c
                    dst = scores[:, n % SBUFS]
                    if kind == 0:
                        last = nc.tensor.matmul(dst[:, off:], k_stack[:, g, P * j:P * j + P],
                                                q_stack[:, b, HG * g + h, off:], start=True, stop=not diagonal)
                    else:
                        last = nc.tensor.matmul(dst[:, off:], k_geo[32 * h:32 * h + GROWS, g, P * j:P * j + P],
                                                q_geo[32 * h:32 * h + GROWS, b, g, off:], start=True, stop=not diagonal)
                    if diagonal:
                        last = nc.tensor.matmul(dst[:, off:off + P], ident_r[:], mask_r[:, 0], start=False, stop=True)
                    last.then_inc(score_full, 1)
                if k in ("values", "sums"):
                    c, g, kind, j = a
                    slot = pv_index[a]
                    off = max(0, j - TPC * c) * P
                    first, end = j == 0, j == TPC * (c + 1) - 1
                    if k == "values":
                        pe.wait_ge(probs_ready, score_index[("score", c, g, kind, j, HG - 1)] + 1)
                        n = epi_index[(c, g, kind)]
                        if first and n >= 1:
                            pe.wait_ge(raw_ready, 2 * n)
                    for h in range(HG):
                        lhs = v_nat[:, j, g] if k == "values" else ones[:, 0:D]
                        last = nc.tensor.matmul(acc[D * h:D * h + D, 0 if k == "values" else 1, off:], lhs,
                                                probs[:, slot % 2, h, off:], start=first, stop=end)
                    if k == "sums":
                        last.then_inc(probs_used, 1)
                if k == "epilogue":
                    pe.wait_ge(probs_used, pv_index[(a[0], a[1], a[2], TPC * (a[0] + 1) - 1)] + 1)
                    pe.nop().then_inc(acc_full, 1)


_INS = ["L0_attn_x", "L0_attn_Wq", "L0_attn_Wk", "L0_attn_Wv", "L0_attn_Wo", "L0_attn_head_scales", "L0_ffn_W_syn",
        "L0_ffn_b_syn", "L0_ffn_W_out", "L0_ffn_b_out", "L0_ffn_gamma", "L0_ffn_beta"]
_OUTS = [((1, T, C), "float32")]


def shape_tables():
    import numpy as np
    inv = np.float32(1.0) / np.float32(10000.0) ** (np.arange(0, D, 2, dtype=np.float32) / np.float32(D))
    f = np.arange(T, dtype=np.float32)[:, None] * inv[None, :].astype(np.float32)
    cos, sin = np.cos(f).astype(np.float32), np.sin(f).astype(np.float32)
    signs = np.array([[sx, sy, sz] for sx in (1.0, -1.0) for sy in (1.0, -1.0) for sz in (1.0, -1.0)], dtype=np.float32)
    ranks = np.arange(1, RANKS + 1, dtype=np.float32)
    return {"cos_table": np.concatenate([cos, cos], axis=1), "sin_table": np.concatenate([-sin, sin], axis=1),
            "small_table": np.concatenate([(signs / np.sqrt(3.0)).astype(np.float32).ravel(), ranks])[None, :]}


def kernel(**inputs):
    import numpy as _np
    import concourse.bacc as _bacc
    from concourse import mybir as _mybir
    from concourse.bass_utils import run_bass_kernel_spmd as _run

    nc = _bacc.Bacc("TRN2", target_bir_lowering=False, num_devices=1)
    arrays, args = {}, []
    for name, a in [(n, inputs[n]) for n in _INS] + list(shape_tables().items()):
        a = _np.ascontiguousarray(a)
        arrays[f"in_{name}_dram"] = a
        args.append(nc.dram_tensor(f"in_{name}_dram", a.shape, _mybir.dt.from_np(a.dtype), kind="ExternalInput").ap())
    for i, (shape, dtype) in enumerate(_OUTS):
        dt = _mybir.dt.from_np(_np.dtype(dtype))
        args.append(nc.dram_tensor(f"out_{i}_dram", shape, dt, kind="ExternalOutput").ap())
    attention_and_ternary_ffn(nc, *args)
    r = _run(nc, [arrays], core_ids=[0])
    return r.results[0]["out_0_dram"]
```
